# Optimizing a Trainium2 kernel written in Bass

```python
import numpy as np
import jax
import jax.numpy as jnp

def _softmax(x, axis=-1):
    return jax.nn.softmax(x, axis=axis)

def _gelu(x):
    return jax.nn.gelu(x, approximate=True)

def _silu(x):
    return jax.nn.silu(x)

def _sigmoid(x):
    return jax.nn.sigmoid(x)

def _layernorm(x, axis=-1, eps=1e-05):
    m = jnp.mean(x, axis=axis, keepdims=True)
    v = jnp.var(x, axis=axis, keepdims=True)
    return (x - m) / jnp.sqrt(v + eps)

def _scatter_add(tgt, idx, src, axis=0):
    return tgt.at[idx].add(src)

def _segment_sum(src, seg, n):
    return jax.ops.segment_sum(src, seg, n)
kernel_name = 'mk_macaron_d1_jaxref_r4_d3e0fe'

def setup_inputs(seed: int=0):
    np.random.seed(seed)
    _w = jnp.asarray

    def _L0_attn_setup():
        import jax, jax.numpy as jnp
        import numpy as np
        B_SZ, T, D_IN, H = (8, 256, 256, 256)
        key = jax.random.key(seed)
        ks = jax.random.split(key, 9)
        lim_u = 1.0 / np.sqrt(D_IN)
        return {'x': jax.random.normal(ks[0], (B_SZ, T, D_IN), dtype=jnp.float32), 'W_u': jax.random.uniform(ks[1], (H, D_IN), jnp.float32, -lim_u, lim_u), 'b_u': jax.random.uniform(ks[2], (H,), jnp.float32, -lim_u, lim_u), 'W_g': jax.random.uniform(ks[3], (H, D_IN), jnp.float32, -lim_u, lim_u), 'b_g': jax.random.uniform(ks[4], (H,), jnp.float32, -lim_u, lim_u), 'A': jnp.eye(H, dtype=jnp.float32) * 0.6, 'Bm': jax.random.normal(ks[5], (H, H), dtype=jnp.float32), 'Cm': jax.random.normal(ks[6], (H, H), dtype=jnp.float32), 'D': jax.random.normal(ks[7], (H,), dtype=jnp.float32)}
    _L0_attn_in = _L0_attn_setup()

    def _L0_ffn_setup():
        import math
        import jax, jax.numpy as jnp
        from jax import lax
        import numpy as np
        E = 16
        K = 2
        CF = 1.25
        key = jax.random.key(seed)
        k0, k1, k2, k3, k4 = jax.random.split(key, 5)
        B, S, D, H = (2, 512, 256, 256)
        scale = 0.02
        return {'x': jax.random.normal(k0, (B, S, D), dtype=jnp.float32), 'router_w': jax.random.normal(k1, (D, E), dtype=jnp.float32) * scale, 'gate_w': jax.random.normal(k2, (E, D, H), dtype=jnp.float32) * scale, 'up_w': jax.random.normal(k3, (E, D, H), dtype=jnp.float32) * scale, 'down_w': jax.random.normal(k4, (E, H, D), dtype=jnp.float32) * scale}
    _L0_ffn_in = _L0_ffn_setup()
    _d = {'L0_attn_x': _L0_attn_in['x'], 'L0_attn_W_u': _L0_attn_in['W_u'], 'L0_attn_b_u': _L0_attn_in['b_u'], 'L0_attn_W_g': _L0_attn_in['W_g'], 'L0_attn_b_g': _L0_attn_in['b_g'], 'L0_attn_A': _L0_attn_in['A'], 'L0_attn_Bm': _L0_attn_in['Bm'], 'L0_attn_Cm': _L0_attn_in['Cm'], 'L0_attn_D': _L0_attn_in['D'], 'L0_ffn_router_w': _L0_ffn_in['router_w'], 'L0_ffn_gate_w': _L0_ffn_in['gate_w'], 'L0_ffn_up_w': _L0_ffn_in['up_w'], 'L0_ffn_down_w': _L0_ffn_in['down_w']}
    _x0 = _d['L0_attn_x']
    _d['L0_attn_x'] = jax.random.normal(jax.random.fold_in(jax.random.key(seed), 1), (4, 2048, 256), dtype=_x0.dtype)
    del _x0
    return _d

def reference(L0_attn_x, L0_attn_W_u, L0_attn_b_u, L0_attn_W_g, L0_attn_b_g, L0_attn_A, L0_attn_Bm, L0_attn_Cm, L0_attn_D, L0_ffn_router_w, L0_ffn_gate_w, L0_ffn_up_w, L0_ffn_down_w):

    def _L0_attn_ref(x, W_u, b_u, W_g, b_g, A, Bm, Cm, D):
        import jax, jax.numpy as jnp
        import numpy as np
        B_SZ, T, D_IN, H = (8, 256, 256, 256)
        u = jax.nn.gelu(jnp.einsum('btd,hd->bth', x, W_u) + b_u, approximate=False) * jax.nn.sigmoid(jnp.einsum('btd,hd->bth', x, W_g) + b_g)
        uB = jnp.einsum('btd,hd->tbh', u, Bm)

        def step(s, uB_t):
            s = s @ A.T + uB_t
            y = s @ Cm.T + D
            return (s, y)
        s0 = jnp.zeros((x.shape[0], A.shape[0]), dtype=x.dtype)
        _, ys = jax.lax.scan(step, s0, uB)
        return jnp.transpose(ys, (1, 0, 2))

    def _L0_ffn_ref(x, router_w, gate_w, up_w, down_w):
        import math
        import jax, jax.numpy as jnp
        from jax import lax
        import numpy as np
        E = 16
        K = 2
        CF = 1.25
        B, S, D = x.shape
        xf = x.reshape(-1, D)
        T = B * S
        capacity = max(1, math.ceil(T * K / E * CF))
        Cbuf = K * capacity
        logits = xf @ router_w
        probs = jax.nn.softmax(logits, axis=-1)
        w, idx = lax.top_k(probs, K)
        oh = jax.nn.one_hot(idx, E, dtype=w.dtype)
        rank = jnp.cumsum(oh, axis=0) - oh
        myrank = jnp.sum(rank * oh, axis=-1)
        keep = myrank < capacity
        w = jnp.where(keep, w, 0.0)
        flat_e = idx.reshape(-1)
        flat_w = w.reshape(-1)
        keep_f = keep.reshape(-1)
        tok = jnp.repeat(jnp.arange(T, dtype=jnp.int32), K)
        ohk = jax.nn.one_hot(flat_e, E, dtype=jnp.int32) * keep_f[:, None].astype(jnp.int32)
        pos = jnp.cumsum(ohk, axis=0) - ohk
        slot = jnp.sum(pos * ohk, axis=-1)
        e_idx = jnp.where(keep_f, flat_e, E)
        dispatch = jnp.full((E + 1, Cbuf), T, dtype=jnp.int32).at[e_idx, slot].set(tok)
        wbuf = jnp.zeros((E + 1, Cbuf), dtype=w.dtype).at[e_idx, slot].set(flat_w)
        dispatch = dispatch[:E]
        wbuf = wbuf[:E]
        x_pad = jnp.concatenate([xf, jnp.zeros((1, D), xf.dtype)], axis=0)
        xe = x_pad[dispatch]
        gate = jnp.einsum('ecd,edh->ech', xe, gate_w)
        up = jnp.einsum('ecd,edh->ech', xe, up_w)
        hidden = jax.nn.silu(gate) * up
        out = jnp.einsum('ech,ehd->ecd', hidden, down_w)
        out = out * wbuf[:, :, None]
        combined = jnp.zeros((T + 1, D), dtype=xf.dtype).at[dispatch.reshape(-1)].add(out.reshape(-1, D))
        return combined[:T].reshape(B, S, D)
    x = L0_attn_x
    x = x + 0.5 * _L0_ffn_ref(_layernorm(x, axis=-1), L0_ffn_router_w, L0_ffn_gate_w, L0_ffn_up_w, L0_ffn_down_w)
    x = x + _L0_attn_ref(_layernorm(x, axis=-1), L0_attn_W_u, L0_attn_b_u, L0_attn_W_g, L0_attn_b_g, L0_attn_A, L0_attn_Bm, L0_attn_Cm, L0_attn_D)
    x = x + 0.5 * _L0_ffn_ref(_layernorm(x, axis=-1), L0_ffn_router_w, L0_ffn_gate_w, L0_ffn_up_w, L0_ffn_down_w)
    return x

_drawn_inputs = setup_inputs


def setup_inputs(seed=0):
    import zlib

    import numpy as np

    out = dict(_drawn_inputs(seed))
    spreads = {}
    factors = {'L0_attn_b_g': 3.414,
     'L0_attn_D': 3.651,
     'L0_ffn_router_w': 8.0,
     'L0_ffn_gate_w': 8.0,
     'L0_ffn_up_w': 8.0,
     'L0_ffn_down_w': 8.0}
    for name, (base, spread) in spreads.items():
        noise = np.random.default_rng([zlib.crc32(name.encode()), seed]).standard_normal(out[name].shape)
        drawn = base * np.exp(spread * noise) if base else spread * noise
        out[name] = jnp.asarray(drawn.astype(out[name].dtype))
    for name, factor in factors.items():
        out[name] = (out[name] * factor).astype(out[name].dtype)
    return out
```

```python
from contextlib import ExitStack

import concourse.bass as bass
from concourse import mybir

ALU = mybir.AluOpType
ACT = mybir.ActivationFunctionType
F32 = mybir.dt.float32
BF16 = mybir.dt.bfloat16
U32 = mybir.dt.uint32
X = mybir.AxisListType.X

P = 128
R = 4
STEPS = 16
D = 256
C = D // P
E = 16
K = 2
TOKENS = 4 * 2048
COLS = R * P
BATCHES = 4
CHUNKS = TOKENS // STEPS // BATCHES
CAPACITY = -(-TOKENS * K * 5 // (E * 4))
REGION = TOKENS
BLOCKS = TOKENS * K // P + E
SLOTS = E * REGION + E * P
NOBODY = 1 << 20
UNDERFLOW = -104.0
EPS = 1e-5
PLAN, KEEP = 5, 8
U = 4
TURNS = BLOCKS // U
LEVELS = CHUNKS.bit_length() - 1
SQUARES = LEVELS + STEPS.bit_length() - 2


def wait(eng, sem, value):
    if not isinstance(value, int) or value > 0:
        eng.wait_ge(sem, value)


def run_steps(eng, tick, total=STEPS, first=2, split=None):
    for i in range(first):
        tick(i, i // 2, i % 2)
    bounds = [first // 2] + ([split // 2] if split else []) + [STEPS // 2]
    for lo, hi in zip(bounds, bounds[1:]):
        with eng.Fori(lo, hi) as t:
            for par in range(2):
                if split:
                    tick(2 * t + par, t, par, hi == split // 2)
                else:
                    tick(2 * t + par, t, par)
    for i in range(STEPS, total):
        tick(i, i // 2, i % 2)


def inside(i, lag):
    return not isinstance(i, int) or 0 <= i - lag < STEPS


def run_blocks(eng, tick, extra, first=1):
    for b in range(U * first):
        tick(b, b // U, b % U)
    with eng.Fori(first, TURNS - 1) as t:
        for u in range(U):
            tick(U * t + u, t, u)
    for u in range(U + extra):
        tick(BLOCKS - U + u, TURNS - 1 + u // U, u % U)


def is_block(b, lag):
    return not isinstance(b, int) or 0 <= b - lag < BLOCKS


def macaron(nc, x, W_u, b_u, W_g, b_g, A, Bm, Cm, Dv, router_w, gate_w, up_w, down_w, out):
    x_v = x.rearrange("b (q r i) d -> i (b q) r d", r=R, i=STEPS)
    out_v = out.rearrange("b (q r i) d -> i (b q) r d", r=R, i=STEPS)

    def dram(name, shape, dt):
        return nc.dram_tensor(name, shape, dt, kind="Internal").ap()

    xn_d = [dram(f"xn_d{f}", [TOKENS, D], F32) for f in range(2)]
    pair_d = [dram(f"pair_d{f}", [TOKENS * K, D], F32) for f in range(2)]
    slot_d = [dram(f"slot_d{f}", [SLOTS, 1], U32) for f in range(2)]
    x1_d = dram("x1_d", [STEPS, P, R * D], F32)
    x2_d = dram("x2_d", [STEPS, P, R * D], F32)
    e_d = dram("e_d", [STEPS, P, C * COLS], F32)
    pow_d = dram("pow_d", [SQUARES, P, C * D], F32)
    xn_v = [t.rearrange("(i p r) d -> i p (r d)", p=P, r=R) for t in xn_d]
    pair_v = [t.rearrange("(i p q) d -> i p (q d)", p=P, q=R * K) for t in pair_d]

    with ExitStack() as ctx:
        def sb(name, shape, dt):
            return ctx.enter_context(nc.sbuf_tensor(name, shape, dt))

        def sem(name):
            return ctx.enter_context(nc.semaphore(name))

        def sems(name, n):
            return [sem(f"{name}{i}") for i in range(n)]

        w_gu = sb("w_gu", [P, C, E, 2 * D], F32)
        w_dn = sb("w_dn", [P, C, E, D], F32)
        r_w = sb("r_w", [P, C, E], F32)
        wT = {n: sb(f"wT_{n}", [P, C, D], F32) for n in ("u", "g", "b", "a", "c")}
        pw = sb("pw", [P, C, D], F32)
        pwT = sb("pwT", [P, C, D], F32)
        level_w = sb("level_w", [P, 2, C, D], F32)
        bias_u = sb("bias_u", [P, C], F32)
        bias_g = sb("bias_g", [P, C], F32)
        d_row = sb("d_row", [P, D], F32)
        ident = sb("ident", [P, P], F32)
        before = sb("before", [P, P], BF16)
        ones = sb("ones", [P, P], BF16)
        reset = sb("reset", [P, K * E, R * STEPS], BF16)
        iota_e = sb("iota_e", [P, E], F32)
        region0 = sb("region0", [P, E], F32)
        pair_no = sb("pair_no", [P, STEPS, R * K], U32)
        steps128 = sb("steps128", [E, REGION // P], F32)
        upto = sb("upto", [E, E], F32)
        ones_e = sb("ones_e", [E, 1], F32)
        block_no = sb("block_no", [E, BLOCKS], F32)
        block_row = sb("block_row", [1, BLOCKS], F32)
        minus_half = sb("minus_half", [P, R], F32)
        key = sb("key", [P, STEPS, R, E], F32)
        key2 = sb("key2", [P, STEPS, R], F32)
        chosen = sb("chosen", [P, K, E, R, STEPS], BF16)
        weight = sb("weight", [P, K, R, STEPS], F32)
        slot_ids = sb("slot_ids", [P, BLOCKS], U32)
        gather_ids = sb("gather_ids", [P, U], U32)
        scatter_ids = sb("scatter_ids", [P, U], U32)
        block_e = sb("block_e", [1, BLOCKS], U32)
        block_r = sb("block_r", [1, BLOCKS], U32)
        stats = sb("stats", [P, R, 6], F32)
        mv = sb("mv", [P, R, 2], F32)
        var = sb("var", [P, R], F32)
        rstd = sb("rstd", [P, R], F32)
        top = sb("top", [P, R], F32)
        key_cur = sb("key_cur", [P, R, E], F32)
        max8 = sb("max8", [P, R, 8], F32)
        idx8 = sb("idx8", [P, R, 8], U32)
        idx_f = sb("idx_f", [P, R, K], F32)
        either = sb("either", [P, R, E], BF16)
        seen = sb("seen", [P, 2, E], BF16)
        added = sb("added", [P, E], F32)
        slot_e = sb("slot_e", [P, R, E], F32)
        slot_k = sb("slot_k", [P, R, K, E], F32)
        slot = sb("slot", [P, 2, R * K], U32)
        pair_cur = sb("pair_cur", [P, 2, R * K], U32)
        count_e = sb("count_e", [E, 1], F32)
        reached = sb("reached", [E, REGION // P], F32)
        blocks_e = sb("blocks_e", [E, 1], F32)
        ends_e = sb("ends_e", [E, 1], F32)
        skip_e = sb("skip_e", [E, 1], F32)
        past = sb("past", [E, BLOCKS], F32)
        incl = sb("incl", [P, K * E, R * STEPS], BF16)
        prefix = sb("prefix", [P, K * E], F32)
        exp2 = sb("exp2", [P, STEPS, R], F32)
        rden = sb("rden", [P, STEPS, R], F32)
        kept = sb("kept", [P, K, R * STEPS], F32)

        work = sb("work", [P, 15 * 1024], F32)

        def part(at, shape):
            n = 1
            for s in shape:
                n *= s
            names = "abcd"[:len(shape)]
            pat = f"p ({' '.join(names)}) -> p {' '.join(names)}"
            return work[:, at:at + n].rearrange(pat, **dict(zip(names, shape)))

        x_in = part(0, [2, R, D])
        pair_in = part(2048, [2, R, K, D])
        xn = part(6144, [2, R, D])
        xnT = part(8192, [C, COLS])
        gelu = part(9216, [C, COLS])
        sig = part(10240, [C, COLS])
        uT = part(12288, [C, COLS])
        e_sb = part(13312, [2, C, COLS])
        e_in = part(2048, [2, C, COLS])
        c_sb = part(4096, [2, C, COLS])
        ends = part(9216, [C, COLS])
        xg = part(9216, [U, D])
        xgT = part(10240, [2, C, P])
        act_g = part(10752, [2, D])
        hid = part(11264, [2, D])
        hidT = part(11776, [2, C, P])
        y_sb = part(12288, [U, D])
        rank = part(2048, [K * E, R * STEPS])
        exps = part(4096, [STEPS * R, E])
        raw = part(11264, [5, C, D])
        empty = part(9216, [1088]).bitcast(U32)

        bank = [ctx.enter_context(nc.psum_tensor(f"bank{i}", [P, 512], F32)) for i in range(8)]

        phase_done = sem("phase_done")
        const_step = sem("const_step")
        table_cleared = sem("table_cleared")
        empty_ready = sem("empty_ready")
        raw_loaded = sem("raw_loaded")
        small_loaded = sem("small_loaded")
        experts_loaded = sem("experts_loaded")
        router_loaded = sem("router_loaded")
        wT_in_psum = sem("wT_in_psum")
        wT_ready = sem("wT_ready")
        x_loaded = sems("x_loaded", 2)
        pair_loaded = sems("pair_loaded", 2)
        e_loaded = sems("e_loaded", 2)
        stats_done = sem("stats_done")
        mv_done = sem("mv_done")
        var_done = sem("var_done")
        rstd_done = sem("rstd_done")
        xn_ready = sem("xn_ready")
        xn_stored = sems("xn_stored", 2)
        xnT_in_psum = sem("xnT_in_psum")
        xnT_ready = sem("xnT_ready")
        logits_done = sem("logits_done")
        top_done = sem("top_done")
        key_done = sem("key_done")
        key_clamped = sem("key_clamped")
        max8_done = sem("max8_done")
        idx8_done = sem("idx8_done")
        idx_f_done = sem("idx_f_done")
        chosen_done = sem("chosen_done")
        either_done = sem("either_done")
        added_done = sem("added_done")
        seen_done = sem("seen_done")
        slots_in_psum = sem("slots_in_psum")
        slot_e_done = sem("slot_e_done")
        slot_k_done = sem("slot_k_done")
        slot_done = sem("slot_done")
        slot_written = sems("slot_written", 2)
        square_in_psum = sem("square_in_psum")
        square_ready = sem("square_ready")
        square_stored = sem("square_stored")
        plan_pe = sem("plan_pe")
        plan_dve = sem("plan_dve")
        keep_pe = sem("keep_pe")
        keep_act = sem("keep_act")
        keep_dve = sem("keep_dve")
        ids_loaded = sems("ids_loaded", U)
        gather_ids_done = sem("gather_ids_done")
        scatter_ids_done = sem("scatter_ids_done")
        xg_loaded = sems("xg_loaded", U)
        xgT_in_psum = sem("xgT_in_psum")
        xgT_ready = sem("xgT_ready")
        gu_in_psum = sem("gu_in_psum")
        act_g_done = sem("act_g_done")
        hid_done = sem("hid_done")
        hidT_in_psum = sem("hidT_in_psum")
        hidT_ready = sem("hidT_ready")
        y_in_psum = sem("y_in_psum")
        y_ready = sem("y_ready")
        y_stored = sems("y_stored", U)
        pair0_added = sem("pair0_added")
        pair1_added = sem("pair1_added")
        x1_ready = sem("x1_ready")
        x1_stored = sems("x1_stored", 2)
        ug_in_psum = sem("ug_in_psum")
        sig_done = sem("sig_done")
        gelu_done = sem("gelu_done")
        uT_ready = sem("uT_ready")
        e_zero = sem("e_zero")
        xg_zero = sem("xg_zero")
        e_in_psum = sem("e_in_psum")
        e_ready = sem("e_ready")
        e_stored = sems("e_stored", 2)
        ends_ready = sem("ends_ready")
        level_loaded = sems("level_loaded", 2)
        level_in_psum = sem("level_in_psum")
        carry_ready = sem("carry_ready")
        c_in_psum = sem("c_in_psum")
        c_ready = sem("c_ready")
        s_ready = sem("s_ready")
        ssm_in_psum = sem("ssm_in_psum")
        x2_ready = sem("x2_ready")
        x2_stored = sems("x2_stored", 2)
        out_ready = sem("out_ready")
        out_stored = sems("out_stored", 2)

        def phase_end(eng, k):
            eng.drain().then_inc(phase_done, 1)
            eng.wait_ge(phase_done, 5 * k)

        def wait_apart(eng, *waits):
            ready = [(sem, v if isinstance(v, int) else eng.compute_val(v)) for sem, v in waits
                     if not isinstance(v, int) or v > 0]
            eng.wait_ge(phase_done, 5)
            for sem, v in ready:
                eng.wait_ge(sem, v)

        LN_ROUTE, LN_SSM = (0, 2 * STEPS), STEPS
        XL_ROUTE, XL_SSM, XL_SECOND, XL_LAST = (16 * n * STEPS // 2 for n in range(4))

        def layernorm(dve, n, par):
            for r in range(R):
                ins = nc.vector.bn_stats(stats[:, r, :], x_in[:, par, r, :])
            ins.then_inc(stats_done, 1)
            wait_apart(dve, (stats_done, n + 1))
            for r in range(R):
                ins = nc.vector.bn_aggr(mv[:, r, :], stats[:, r, :])
            ins.then_inc(mv_done, 1)
            dve.wait_ge(mv_done, n + 1)
            wait(dve, rstd_done, n)
            nc.vector.tensor_scalar(var[:], mv[:, :, 1], EPS, None, ALU.add).then_inc(var_done, 1)
            wait(dve, xnT_in_psum, n - 1)
            dve.wait_ge(rstd_done, n + 1)

        def normalize(dve, n, par):
            for r in range(R):
                ins = nc.vector.tensor_scalar(xn[:, par, r, :], x_in[:, par, r, :], mv[:, r, 0:1],
                                              rstd[:, r:r + 1], ALU.subtract, ALU.mult)
            ins.then_inc(xn_ready, 1)

        def rstd_step(pool, n):
            pool.wait_ge(var_done, n + 1)
            wait(pool, xn_ready, n)
            nc.gpsimd.tensor_tensor(rstd[:], var[:], minus_half[:], ALU.pow).then_inc(rstd_done, 1)

        def turn_xn(pe, n, par):
            pe.wait_ge(xn_ready, n + 1)
            wait(pe, xnT_ready, n)
            for c in range(C):
                for r in range(R):
                    ins = nc.tensor.transpose(bank[c][:, r * P:(r + 1) * P],
                                              xn[:, par, r, c * P:(c + 1) * P], ident[:])
            ins.then_inc(xnT_in_psum, 1)

        def copy_xnT(act, n, users, used):
            act.wait_ge(xnT_in_psum, n + 1)
            wait(act, users, used)
            for c in range(C):
                ins = nc.scalar.copy(xnT[:, c, :], bank[c][:])
            ins.then_inc(xnT_ready, 1)

        def flat(ap):
            names = "abcd"[:len(ap.shape) - 1]
            return ap.rearrange(f"p {' '.join(names)} -> p ({' '.join(names)})")

        block = ctx.enter_context(nc.Block())

        @block.sync
        def _(sp):
            for n, w in enumerate((W_u, W_g, Bm, A, Cm)):
                sp.dma_start(raw[:, n], w.rearrange("(c p) d -> p c d", p=P)).then_inc(raw_loaded, 16)
            sp.dma_start(pw[:], A.rearrange("(c p) d -> p c d", p=P)).then_inc(raw_loaded, 16)
            sp.dma_start(r_w[:], router_w.rearrange("(c p) e -> p c e", p=P)).then_inc(router_loaded, 16)
            for dst, b in ((bias_u, b_u), (bias_g, b_g)):
                for c in range(C):
                    sp.dma_start(dst[:, c:c + 1],
                                 b.rearrange("(c p a) -> c p a", p=P, a=1)[c]).then_inc(small_loaded, 16)
            sp.dma_start(d_row[:], Dv.rearrange("(a d) -> a d", a=1).broadcast_to([P, D])).then_inc(small_loaded, 16)
            sp.wait_ge(empty_ready, 1)
            for f in range(2):
                sp.dma_start(slot_d[f].rearrange("(p s) a -> p (s a)", p=P),
                             empty[:, 0:SLOTS // P]).then_inc(table_cleared, 16)
            sp.wait_ge(table_cleared, 32)
            phase_end(sp, 1)

            def load_x(i, t, par):
                wait(sp, xn_ready, i - 1)
                sp.dma_start(x_in[:, par], x_v[i]).then_inc(x_loaded[par], 16)

            run_steps(sp, load_x)
            phase_end(sp, 2)

            def load_ids(f):
                sp.wait_ge(plan_dve, PLAN * (f + 1))

                def load(b, t, u):
                    if f or not isinstance(b, int) or b >= U:
                        wait_apart(sp, (ids_loaded[u], 16 * (f * TURNS + t)))
                    row = sp.value_load(block_r[0:1, bass.ds(b, 1)], min_val=0, max_val=SLOTS - P)
                    sp.dma_start(slot_ids[:, bass.ds(b, 1)],
                                 slot_d[f][bass.ds(row, P), :]).then_inc(ids_loaded[u], 16)

                run_blocks(sp, load, 0)

            load_ids(0)
            phase_end(sp, 3)

            def load_ssm(i, t, par):
                wait(sp, x1_stored[par], 16 * t)
                sp.dma_start(x_in[:, par], x_v[i]).then_inc(x_loaded[par], 16)
                wait(sp, pair1_added, i - 1)
                sp.dma_start(flat(pair_in[:, par]), pair_v[0][i]).then_inc(pair_loaded[par], 16)

            run_steps(sp, load_ssm)
            phase_end(sp, 4)
            for k in range(LEVELS):
                wait(sp, level_in_psum, k - 1)
                sp.dma_start(flat(level_w[:, k % 2]), pow_d[SQUARES - LEVELS + k]).then_inc(level_loaded[k % 2], 16)
            phase_end(sp, 5)

            def second_pass(i, t, par):
                if inside(i, 2):
                    sp.wait_ge(x2_ready, i - 1)
                    sp.dma_start(x2_d[i - 2], flat(x_in[:, par])).then_inc(x2_stored[par], 16)
                if inside(i, 0):
                    wait(sp, ssm_in_psum, i - 1)
                    sp.dma_start(flat(e_in[:, par]), e_d[i]).then_inc(e_loaded[par], 16)
                    if inside(i, 2):
                        wait_apart(sp, (x2_stored[par], 16 * t),
                                   (xn_ready, LN_ROUTE[1] + i - 1))
                    sp.dma_start(flat(x_in[:, par]), x1_d[i]).then_inc(x_loaded[par], 16)

            run_steps(sp, second_pass, STEPS + 2)
            for par in range(2):
                sp.wait_ge(x2_stored[par], 8 * STEPS)
            phase_end(sp, 6)
            load_ids(1)
            phase_end(sp, 7)

            def last_pass(i, t, par):
                if inside(i, 2):
                    sp.wait_ge(out_ready, i - 1)
                    sp.dma_start(out_v[i - 2], x_in[:, par]).then_inc(out_stored[par], 16)
                if inside(i, 0):
                    sp.dma_start(flat(pair_in[:, par]), pair_v[1][i]).then_inc(pair_loaded[par], 16)
                    if inside(i, 2):
                        sp.wait_ge(out_stored[par], 16 * t)
                    sp.dma_start(flat(x_in[:, par]), x2_d[i]).then_inc(x_loaded[par], 16)

            run_steps(sp, last_pass, STEPS + 2)
            for par in range(2):
                sp.wait_ge(out_stored[par], 8 * STEPS)

        @block.gpsimd
        def _(pool):
            nc.gpsimd.memset(empty[:], NOBODY).then_inc(empty_ready, 1)
            nc.gpsimd.memset(ident[:], 0.0)
            nc.gpsimd.memset(ones[:], 1.0)
            nc.gpsimd.memset(upto[:], 1.0)
            nc.gpsimd.memset(ones_e[:], 1.0)
            nc.gpsimd.memset(minus_half[:], -0.5)
            nc.gpsimd.memset(seen[:, 0], 0.0)
            nc.gpsimd.memset(before[:], 1.0)
            nc.gpsimd.memset(reset[:], 1.0).then_inc(const_step, 1)
            pool.wait_ge(const_step, 1)
            nc.gpsimd.affine_select(out=ident[:], in_=ident[:], compare_op=ALU.not_equal, fill=1.0,
                                    base=0, pattern=[[-1, P]], channel_multiplier=1)
            nc.gpsimd.affine_select(out=before[:], in_=before[:], compare_op=ALU.is_gt, fill=0.0,
                                    base=0, pattern=[[1, P]], channel_multiplier=-1)
            nc.gpsimd.affine_select(out=upto[:], in_=upto[:], compare_op=ALU.is_ge, fill=0.0,
                                    base=0, pattern=[[1, E]], channel_multiplier=-1)
            nc.gpsimd.memset(reset[:, :, 0:1], 0.0)
            nc.gpsimd.iota(iota_e[:], pattern=[[1, E]], base=0, channel_multiplier=0,
                           allow_small_or_imprecise_dtypes=True)
            nc.gpsimd.iota(region0[:], pattern=[[REGION, E]], base=0, channel_multiplier=0,
                           allow_small_or_imprecise_dtypes=True)
            nc.gpsimd.iota(pair_no[:], pattern=[[COLS * K, STEPS], [1, R * K]], base=0,
                           channel_multiplier=R * K)
            nc.gpsimd.iota(steps128[:], pattern=[[P, REGION // P]], base=0, channel_multiplier=0,
                           allow_small_or_imprecise_dtypes=True)
            nc.gpsimd.iota(block_no[:], pattern=[[1, BLOCKS]], base=0, channel_multiplier=0,
                           allow_small_or_imprecise_dtypes=True)
            nc.gpsimd.iota(block_row[:], pattern=[[P, BLOCKS]], base=0, channel_multiplier=0,
                           allow_small_or_imprecise_dtypes=True)
            phase_end(pool, 1)

            def write_slots(f, i, par):
                wait_apart(pool, (slot_done, STEPS * f + i + 1))
                for q in range(R * K):
                    nc.gpsimd.indirect_dma_start(
                        out=slot_d[f], out_offset=bass.IndirectOffsetOnAxis(ap=slot[:, par, q:q + 1], axis=0),
                        in_=pair_cur[:, par, q:q + 1], in_offset=None).then_inc(slot_written[par], 16)

            def all_written(f):
                for par in range(2):
                    pool.wait_ge(slot_written[par], 16 * R * K * (STEPS // 2) * (f + 1))

            def route0(i, t, par):
                if inside(i, 0):
                    rstd_step(pool, LN_ROUTE[0] + i)
                if inside(i, 1):
                    write_slots(0, i - 1, 1 - par)

            run_steps(pool, route0, STEPS + 1)
            all_written(0)
            phase_end(pool, 2)

            def experts(f):
                nc.gpsimd.memset(xg[:], 0.0).then_inc(xg_zero, 1)
                pool.wait_ge(xg_zero, f + 1)

                def tick(b, t, u):
                    n = BLOCKS * f + b
                    if is_block(b, 0):
                        wait_apart(pool, (gather_ids_done, n + 1),
                                         (xgT_in_psum, n - U + 1))
                        nc.gpsimd.indirect_dma_start(
                            out=xg[:, u], out_offset=None, in_=xn_d[f],
                            in_offset=bass.IndirectOffsetOnAxis(ap=gather_ids[:, u:u + 1], axis=0),
                            bounds_check=TOKENS - 1, oob_is_err=False).then_inc(xg_loaded[u], 16)
                    if is_block(b, 3):
                        v = (u + 1) % U
                        wait_apart(pool, (scatter_ids_done, n - 2),
                                         (y_ready, n - 2))
                        nc.gpsimd.indirect_dma_start(
                            out=pair_d[f],
                            out_offset=bass.IndirectOffsetOnAxis(ap=scatter_ids[:, v:v + 1], axis=0),
                            in_=y_sb[:, v], in_offset=None,
                            bounds_check=TOKENS * K - 1, oob_is_err=False).then_inc(y_stored[v], 16)

                run_blocks(pool, tick, 3)
                for u in range(U):
                    pool.wait_ge(y_stored[u], 16 * TURNS * (f + 1))

            experts(0)
            phase_end(pool, 3)

            def ssm_input(i, t, par):
                rstd_step(pool, LN_SSM + i)
                pool.wait_ge(xn_ready, LN_SSM + i + 1)
                nc.gpsimd.tensor_tensor(x_in[:, par], x_in[:, par],
                                        d_row[:].unsqueeze(1).broadcast_to([P, R, D]),
                                        ALU.add).then_inc(x1_ready, 1)
                wait_apart(pool, (x1_ready, i + 1))
                pool.dma_start(x1_d[i], flat(x_in[:, par])).then_inc(x1_stored[par], 16)

            run_steps(pool, ssm_input)
            for par in range(2):
                pool.wait_ge(x1_stored[par], 8 * STEPS)
            phase_end(pool, 4)
            phase_end(pool, 5)

            def second_pass(i, t, par):
                if inside(i, 1):
                    rstd_step(pool, LN_ROUTE[1] + i - 1)
                if inside(i, 3):
                    write_slots(1, i - 3, 1 - par)

            run_steps(pool, second_pass, STEPS + 3, first=4)
            all_written(1)
            phase_end(pool, 6)
            experts(1)
            phase_end(pool, 7)

        @block.scalar
        def _(act):
            act.wait_ge(small_loaded, 80)
            phase_end(act, 1)
            for c in range(C):
                rows = slice(c * P, (c + 1) * P)
                for es in (slice(0, E // 2), slice(E // 2, E)):
                    for dst, w in ((w_gu[:, c, es, 0:D], gate_w), (w_gu[:, c, es, D:], up_w), (w_dn[:, c, es, :], down_w)):
                        act.dma_start(dst, w[es, rows, :].rearrange("e p h -> p e h")).then_inc(experts_loaded, 16)
            for n, name in enumerate("ugbac"):
                act.wait_ge(wT_in_psum, n + 1)
                nc.scalar.copy(flat(wT[name][:]), bank[n][:]).then_inc(wT_ready, 1)
            nc.scalar.copy(flat(pwT[:]), bank[3][:]).then_inc(wT_ready, 1)

            def store_xn(f, i, par):
                act.wait_ge(xn_ready, LN_ROUTE[f] + i + 1)
                act.dma_start(xn_v[f][i], flat(xn[:, par])).then_inc(xn_stored[par], 16)

            def route0(i, t, par, squares=True):
                if inside(i, 0):
                    store_xn(0, i, par)
                    copy_xnT(act, LN_ROUTE[0] + i, logits_done, i)
                if inside(i, 0) and squares:
                    act.wait_ge(square_in_psum, i + 1)
                    wait(act, square_stored, 16 * i)
                    nc.scalar.copy(flat(pw[:]), bank[4][:])
                    nc.scalar.copy(flat(pwT[:]), bank[5][:]).then_inc(square_ready, 1)
                    act.wait_ge(square_ready, i + 1)
                    act.dma_start(pow_d[i], flat(pwT[:])).then_inc(square_stored, 16)

            run_steps(act, route0, split=SQUARES)
            act.wait_ge(square_stored, 16 * SQUARES)
            for par in range(2):
                act.wait_ge(xn_stored[par], 8 * STEPS)
            phase_end(act, 2)

            def experts(f):
                N = BLOCKS * f
                nc.scalar.activation(exps[:], key[:].rearrange("p i r e -> p (i r) e"), ACT.Exp)
                nc.scalar.activation(exp2[:], key2[:], ACT.Exp).then_inc(keep_act, 1)

                def copy_xgT(b, par):
                    act.wait_ge(xgT_in_psum, N + b + 1)
                    wait(act, gu_in_psum, N + b - 1)
                    nc.scalar.copy(flat(xgT[:, par]), bank[0][:, 0:D]).then_inc(xgT_ready, 1)

                def tick(b, t, u):
                    if is_block(b, -1):
                        copy_xgT(b + 1, (u + 1) % 2)
                    if is_block(b, 0):
                        act.wait_ge(gu_in_psum, N + b + 1)
                        wait(act, hid_done, N + b - 1)
                        nc.scalar.activation(act_g[:, u % 2], bank[2 + u % 2][:, 0:D],
                                             ACT.Silu).then_inc(act_g_done, 1)
                    if is_block(b, 1):
                        v = (u + U - 1) % U
                        act.wait_ge(y_in_psum, N + b)
                        wait(act, y_stored[v], 16 * (TURNS * f + t - (u == 0)))
                        nc.scalar.copy(y_sb[:, v], bank[4 + v % 2][:, 0:D]).then_inc(y_ready, 1)

                copy_xgT(0, 0)
                run_blocks(act, tick, 1, first=2)

            experts(0)
            phase_end(act, 3)

            def ssm_input(i, t, par):
                if inside(i, 1):
                    act.wait_ge(ug_in_psum, i)
                    wait(act, uT_ready, i - 1)
                    for m in range(C):
                        ins = nc.scalar.activation(gelu[:, m, :], bank[2 + m][:], ACT.Gelu,
                                                   bias=bias_u[:, m:m + 1])
                    ins.then_inc(gelu_done, 1)
                    for m in range(C):
                        ins = nc.scalar.activation(sig[:, m, :], bank[4 + m][:], ACT.Sigmoid,
                                                   bias=bias_g[:, m:m + 1])
                    ins.then_inc(sig_done, 1)
                if inside(i, 2):
                    act.wait_ge(e_in_psum, i - 1)
                    wait(act, e_stored[par], 16 * (t - 1))
                    for m in range(C):
                        ins = nc.scalar.copy(e_sb[:, par, m, :], bank[6 + m][:])
                    ins.then_inc(e_ready, 1)
                    act.wait_ge(e_ready, i - 1)
                    act.dma_start(e_d[i - 2], flat(e_sb[:, par])).then_inc(e_stored[par], 16)
                if inside(i, 0):
                    copy_xnT(act, LN_SSM + i, ug_in_psum, i)

            run_steps(act, ssm_input, STEPS + 2, first=4)
            for par in range(2):
                act.wait_ge(e_stored[par], 8 * STEPS)
            phase_end(act, 4)
            phase_end(act, 5)

            def second_pass(i, t, par):
                if inside(i, 0):
                    act.wait_ge(c_in_psum, i + 1)
                    wait(act, s_ready, i - 1)
                    for m in range(C):
                        ins = nc.scalar.copy(c_sb[:, par, m, :], bank[4 + m][:])
                    ins.then_inc(c_ready, 1)
                if inside(i, 2):
                    store_xn(1, i - 2, par)
                    copy_xnT(act, LN_ROUTE[1] + i - 2, logits_done, STEPS + i - 2)

            run_steps(act, second_pass, STEPS + 2)
            for par in range(2):
                act.wait_ge(xn_stored[par], 16 * STEPS)
            phase_end(act, 6)
            experts(1)
            phase_end(act, 7)

        @block.tensor
        def _(pe):
            pe.wait_ge(raw_loaded, 96)
            phase_end(pe, 1)
            for n in range(5):
                for k in range(C):
                    for m in range(C):
                        ins = nc.tensor.transpose(bank[n][:, k * D + m * P:k * D + (m + 1) * P],
                                                  raw[:, n, m, k * P:(k + 1) * P], ident[:])
                ins.then_inc(wT_in_psum, 1)
            pe.wait_ge(wT_ready, 6)
            pe.wait_ge(router_loaded, 16)

            def product(out_of, lhs, rhs, m_range=range(C)):
                for m in m_range:
                    for c in range(C):
                        ins = nc.tensor.matmul(out_of(m), lhs(c, m), rhs(c), start=(c == 0), stop=(c == C - 1))
                return ins

            def route_logits(f, i):
                pe.wait_ge(xnT_ready, LN_ROUTE[f] + i + 1)
                wait(pe, key_done, STEPS * f + i)
                for r in range(R):
                    for c in range(C):
                        ins = nc.tensor.matmul(bank[2][:, r * E:(r + 1) * E], xnT[:, c, r * P:(r + 1) * P],
                                               r_w[:, c, :], start=(c == 0), stop=(c == C - 1))
                ins.then_inc(logits_done, 1)

            def route_slots(f, i, par):
                n = STEPS * f + i
                pe.wait_ge(either_done, n + 1)
                wait(pe, seen_done, n)
                wait(pe, slot_e_done, n)
                place = bank[3][:, 0:R * E].rearrange("p (r e) -> p r e", r=R)
                nc.tensor.matmul(place, before[:], either[:], start=True, stop=False)
                for r in range(R - 1):
                    nc.tensor.matmul(place[:, r + 1:, :], ones[:],
                                     either[:, r:r + 1, :].broadcast_to([P, R - 1 - r, E]),
                                     start=False, stop=False)
                nc.tensor.matmul(place, ones[:], seen[:, par].unsqueeze(1).broadcast_to([P, R, E]),
                                 start=False, stop=True).then_inc(slots_in_psum, 1)

            def route0(i, t, par, squares=True):
                if inside(i, 0):
                    turn_xn(pe, LN_ROUTE[0] + i, par)
                    if squares:
                        wait(pe, square_ready, i)
                        product(lambda m: bank[4][:, m * D:(m + 1) * D],
                                lambda c, m: pwT[:, c, m * P:(m + 1) * P], lambda c: pw[:, c, :])
                        product(lambda m: bank[5][:, m * D:(m + 1) * D],
                                lambda c, m: pw[:, c, m * P:(m + 1) * P],
                                lambda c: pwT[:, c, :]).then_inc(square_in_psum, 1)
                    route_logits(0, i)
                if inside(i, 1):
                    route_slots(0, i - 1, 1 - par)

            run_steps(pe, route0, STEPS + 1, split=SQUARES)
            phase_end(pe, 2)

            def plan(f):
                at = PLAN * f
                nc.tensor.matmul(bank[2][0:E, 0:1], seen[:, 0], ones[:, 0:1], start=True,
                                 stop=True).then_inc(plan_pe, 1)
                pe.wait_ge(plan_dve, at + 2)
                nc.tensor.matmul(bank[3][0:E, 0:1], upto[:], blocks_e[:], start=True,
                                 stop=True).then_inc(plan_pe, 1)
                pe.wait_ge(plan_dve, at + 4)
                nc.tensor.matmul(bank[2][0:1, 0:BLOCKS], ones_e[:], past[:], start=True, stop=True)
                nc.tensor.matmul(bank[3][0:1, 0:BLOCKS], skip_e[:], past[:], start=True,
                                 stop=True).then_inc(plan_pe, 1)
                pe.wait_ge(keep_dve, KEEP * f + 1)
                nc.tensor.matmul(bank[4][:, 0:K * E], before[:], incl[:, :, R * STEPS - 1], start=True,
                                 stop=True).then_inc(keep_pe, 1)
                pe.wait_ge(keep_dve, KEEP * f + 2)
                pe.wait_ge(plan_dve, at + PLAN)

            def experts(f):
                N = BLOCKS * f
                pe.wait_ge(experts_loaded, 16 * 12)

                def turn_xg(b, t, u):
                    pe.wait_ge(xg_loaded[u], 16 * (TURNS * f + t + 1))
                    wait(pe, xgT_ready, N + b)
                    for c in range(C):
                        ins = nc.tensor.transpose(bank[0][:, c * P:(c + 1) * P], xg[:, u, c * P:(c + 1) * P], ident[:])
                    ins.then_inc(xgT_in_psum, 1)

                def tick(b, t, u):
                    par, last = u % 2, (u + 1) % 2
                    if is_block(b, 0):
                        e = pe.value_load(block_e[0:1, bass.ds(b, 1)], min_val=0, max_val=E - 1)
                        pe.wait_ge(xgT_ready, N + b + 1)
                        wait(pe, hid_done, N + b - 1)
                        nc.tensor.matmul(bank[2 + par][:], xgT[:, par, 0, :], w_gu[:, 0, e, :],
                                         start=True, stop=False)
                    if is_block(b, 1):
                        pe.wait_ge(hid_done, N + b)
                        wait(pe, hidT_ready, N + b - 1)
                        for c in range(C):
                            ins = nc.tensor.transpose(bank[1][:, c * P:(c + 1) * P],
                                                      hid[:, last, c * P:(c + 1) * P], ident[:])
                        ins.then_inc(hidT_in_psum, 1)
                    if is_block(b, -1):
                        turn_xg(b + 1, t + (u + 1) // U, (u + 1) % U)
                    if is_block(b, 0):
                        nc.tensor.matmul(bank[2 + par][:], xgT[:, par, 1, :], w_gu[:, 1, e, :],
                                         start=False, stop=True).then_inc(gu_in_psum, 1)
                    if is_block(b, 1):
                        e = pe.value_load(block_e[0:1, bass.ds(b - 1, 1)], min_val=0, max_val=E - 1)
                        pe.wait_ge(hidT_ready, N + b)
                        wait(pe, y_ready, N + b - 2)
                        for c in range(C):
                            ins = nc.tensor.matmul(bank[4 + last][:, 0:D], hidT[:, last, c, :], w_dn[:, c, e, :],
                                                   start=(c == 0), stop=(c == C - 1))
                        ins.then_inc(y_in_psum, 1)

                turn_xg(0, 0, 0)
                run_blocks(pe, tick, 1)

            plan(0)
            experts(0)
            phase_end(pe, 3)
            pe.wait_ge(e_zero, 1)

            def weight_of(name):
                return lambda c, m: wT[name][:, c, m * P:(m + 1) * P]

            def ssm_input(i, t, par):
                if inside(i, 1):
                    pe.wait_ge(xnT_ready, LN_SSM + i)
                    wait(pe, gelu_done, i - 1)
                    wait(pe, sig_done, i - 1)
                    product(lambda m: bank[2 + m][:], weight_of("u"), lambda c: xnT[:, c, :])
                    product(lambda m: bank[4 + m][:], weight_of("g"),
                            lambda c: xnT[:, c, :]).then_inc(ug_in_psum, 1)
                if inside(i, 2):
                    pe.wait_ge(uT_ready, i - 1)
                    wait(pe, e_ready, i - 2)
                    for m in range(C):
                        for c in range(C):
                            nc.tensor.matmul(bank[6 + m][:], weight_of("b")(c, m), uT[:, c, :],
                                             start=(c == 0), stop=False)
                        for c in range(C):
                            ins = nc.tensor.matmul(bank[6 + m][:], weight_of("a")(c, m), e_sb[:, 1 - par, c, :],
                                                   start=False, stop=(c == C - 1))
                    ins.then_inc(e_in_psum, 1)
                if inside(i, 0):
                    turn_xn(pe, LN_SSM + i, par)

            run_steps(pe, ssm_input, STEPS + 2, first=4)
            phase_end(pe, 4)
            for k in range(LEVELS):
                width = CHUNKS - 2 ** k
                pe.wait_ge(ends_ready, k + 1)
                pe.wait_ge(level_loaded[k % 2], 16 * (k // 2 + 1))
                for m in range(C):
                    for c in range(C):
                        ins = nc.tensor.matmul(
                            bank[6 + m][:, 0:BATCHES * width].rearrange("p (b n) -> p b n", b=BATCHES),
                            level_w[:, k % 2, c, m * P:(m + 1) * P],
                            ends[:, c, :].rearrange("p (b n) -> p b n", b=BATCHES)[:, :, 0:width],
                            start=(c == 0), stop=(c == C - 1))
                ins.then_inc(level_in_psum, 1)
            phase_end(pe, 5)
            pe.wait_ge(carry_ready, 1)

            def second_pass(i, t, par):
                last = 1 - par
                if inside(i, 1):
                    pe.wait_ge(s_ready, i)
                    wait(pe, x2_ready, i - 1)
                    for r in range(R):
                        for c in range(C):
                            ins = nc.tensor.matmul(bank[6 + r // 2][:, (r % 2) * D:(r % 2 + 1) * D],
                                                   e_in[:, last, c, r * P:(r + 1) * P], wT["c"][:, c, :],
                                                   start=(c == 0), stop=(c == C - 1))
                    ins.then_inc(ssm_in_psum, 1)
                if inside(i, 0):
                    wait(pe, c_ready, i)
                    product(lambda m: bank[4 + m][:], weight_of("a"),
                            lambda c: c_sb[:, last, c, :]).then_inc(c_in_psum, 1)
                if inside(i, 2):
                    turn_xn(pe, LN_ROUTE[1] + i - 2, par)
                    route_logits(1, i - 2)
                if inside(i, 3):
                    route_slots(1, i - 3, last)

            run_steps(pe, second_pass, STEPS + 3, first=4)
            phase_end(pe, 6)
            plan(1)
            experts(1)
            phase_end(pe, 7)

        @block.vector
        def _(dve):
            phase_end(dve, 1)

            def route(f, i, par):
                n = STEPS * f + i
                lg = bank[2][:, 0:R * E].rearrange("p (r e) -> p r e", r=R)
                dve.wait_ge(logits_done, n + 1)
                nc.vector.tensor_reduce(top[:], lg, X, ALU.max).then_inc(top_done, 1)
                dve.wait_ge(top_done, n + 1)
                nc.vector.tensor_tensor(key_cur[:], lg, top[:].unsqueeze(2).broadcast_to([P, R, E]),
                                        ALU.subtract).then_inc(key_done, 1)
                dve.wait_ge(key_done, n + 1)
                nc.vector.tensor_scalar(key_cur[:], key_cur[:], UNDERFLOW, None, ALU.max).then_inc(key_clamped, 1)
                wait_apart(dve, (key_clamped, n + 1))
                for r in range(R):
                    ins = nc.vector.max(max8[:, r, :], key_cur[:, r, :])
                ins.then_inc(max8_done, 1)
                wait_apart(dve, (max8_done, n + 1))
                for r in range(R):
                    ins = nc.vector.max_index(idx8[:, r, :], max8[:, r, :], key_cur[:, r, :])
                ins.then_inc(idx8_done, 1)
                nc.vector.tensor_copy(key[:, i], key_cur[:])
                nc.vector.tensor_copy(key2[:, i], max8[:, :, 1])
                dve.wait_ge(idx8_done, n + 1)
                nc.vector.tensor_copy(idx_f[:], idx8[:, :, 0:K]).then_inc(idx_f_done, 1)
                dve.wait_ge(idx_f_done, n + 1)
                for k in range(K):
                    picked = chosen[:, k, :, :, i].rearrange("p e r -> p r e")
                    ins = nc.vector.tensor_tensor(picked, idx_f[:, :, k:k + 1].broadcast_to([P, R, E]),
                                                  iota_e[:].unsqueeze(1).broadcast_to([P, R, E]), ALU.is_equal)
                ins.then_inc(chosen_done, 1)
                dve.wait_ge(chosen_done, n + 1)
                wait(dve, slots_in_psum, n)
                nc.vector.tensor_tensor(either[:], chosen[:, 0, :, :, i].rearrange("p e r -> p r e"),
                                        chosen[:, 1, :, :, i].rearrange("p e r -> p r e"),
                                        ALU.add).then_inc(either_done, 1)
                dve.wait_ge(either_done, n + 1)
                nc.vector.tensor_reduce(added[:], either[:].rearrange("p r e -> p e r"), X,
                                        ALU.add).then_inc(added_done, 1)
                dve.wait_ge(added_done, n + 1)
                nc.vector.tensor_tensor(seen[:, 1 - par], seen[:, par], added[:], ALU.add).then_inc(seen_done, 1)
                dve.wait_ge(slots_in_psum, n + 1)
                nc.vector.tensor_tensor(slot_e[:], bank[3][:, 0:R * E].rearrange("p (r e) -> p r e", r=R),
                                        region0[:].unsqueeze(1).broadcast_to([P, R, E]),
                                        ALU.add).then_inc(slot_e_done, 1)
                dve.wait_ge(slot_e_done, n + 1)
                for k in range(K):
                    ins = nc.vector.tensor_tensor(slot_k[:, :, k, :],
                                                  chosen[:, k, :, :, i].rearrange("p e r -> p r e"),
                                                  slot_e[:], ALU.mult)
                ins.then_inc(slot_k_done, 1)
                dve.wait_ge(slot_k_done, n + 1)

            def send(f, i, t, par):
                wait_apart(dve, (slot_written[par], 16 * R * K * (STEPS // 2 * f + t)))
                nc.vector.tensor_copy(pair_cur[:, par], pair_no[:, i])
                with nc.allow_low_precision(reason="slot numbers are integers below 2^24"):
                    nc.vector.tensor_reduce(slot[:, par], slot_k[:].rearrange("p r k e -> p (r k) e"), X,
                                            ALU.add).then_inc(slot_done, 1)

            def route0(i, t, par):
                if inside(i, 0):
                    dve.wait_ge(x_loaded[par], XL_ROUTE + 16 * (t + 1))
                    layernorm(dve, LN_ROUTE[0] + i, par)
                    if inside(i, 2):
                        dve.wait_ge(xn_stored[par], 16 * t)
                    normalize(dve, LN_ROUTE[0] + i, par)
                if inside(i, 1):
                    route(0, i - 1, 1 - par)
                    send(0, i - 1, t - 1 + par, 1 - par)

            run_steps(dve, route0, STEPS + 1, first=4)
            phase_end(dve, 2)

            def plan(f):
                at = PLAN * f

                def step(k, ins):
                    ins.then_inc(plan_dve, 1)
                    dve.wait_ge(plan_dve, at + k)

                dve.wait_ge(plan_pe, 3 * f + 1)
                step(1, nc.vector.tensor_copy(count_e[:], bank[2][0:E, 0:1]))
                step(2, nc.vector.tensor_scalar(reached[:], steps128[:], count_e[:], 0.0, ALU.is_lt, ALU.add,
                                                accum_out=blocks_e[:]))
                nc.vector.tensor_scalar(skip_e[:], blocks_e[:], -float(P), float(REGION), ALU.mult, ALU.add)
                dve.wait_ge(plan_pe, 3 * f + 2)
                step(3, nc.vector.tensor_copy(ends_e[:], bank[3][0:E, 0:1]))
                step(4, nc.vector.tensor_scalar(past[:], block_no[:], ends_e[:], None, ALU.is_ge))
                dve.wait_ge(plan_pe, 3 * f + 3)
                nc.vector.tensor_scalar(block_e[:], bank[2][0:1, 0:BLOCKS], float(E - 1), None, ALU.min)
                step(5, nc.vector.tensor_tensor(block_r[:], bank[3][0:1, 0:BLOCKS], block_row[:], ALU.add))
                nc.vector.memset(seen[:, 0], 0.0)

            def keep(f):
                def step(k, ins):
                    ins.then_inc(keep_dve, 1)
                    dve.wait_ge(keep_dve, KEEP * f + k)

                every = flat(chosen[:])
                step(1, nc.vector.tensor_tensor_scan(flat(incl[:]), flat(reset[:]), every, 0.0, ALU.mult, ALU.add))
                dve.wait_ge(keep_pe, f + 1)
                step(2, nc.vector.tensor_copy(prefix[:], bank[4][:, 0:K * E]))
                step(3, nc.vector.tensor_tensor(rank[:], incl[:],
                                                prefix[:].unsqueeze(2).broadcast_to([P, K * E, R * STEPS]), ALU.add))
                step(4, nc.vector.scalar_tensor_tensor(out=flat(rank[:]), in0=flat(rank[:]), scalar=float(CAPACITY),
                                                       in1=every, op0=ALU.is_le, op1=ALU.mult))
                nc.vector.tensor_reduce(kept[:], rank[:].rearrange("p (k e) j -> p k j e", k=K), X, ALU.add)
                dve.wait_ge(keep_act, f + 1)
                step(5, nc.vector.tensor_reduce(rden[:].rearrange("p i r -> p (i r)"), exps[:], X, ALU.add))
                step(6, nc.vector.reciprocal(rden[:], rden[:]))

                def of(k):
                    return (weight[:, k].rearrange("p r i -> p i r"),
                            kept[:, k].rearrange("p (r i) -> p i r", r=R))

                w, kp = of(0)
                nc.vector.scalar_tensor_tensor(out=w, in0=rden[:], scalar=0.5, in1=kp, op0=ALU.mult, op1=ALU.mult)
                step(7, nc.vector.tensor_tensor(exp2[:], exp2[:], rden[:], ALU.mult))
                w, kp = of(1)
                step(8, nc.vector.scalar_tensor_tensor(out=w, in0=exp2[:], scalar=0.5, in1=kp,
                                                       op0=ALU.mult, op1=ALU.mult))

            def experts(f):
                N = BLOCKS * f

                def to_gather(b, t, u):
                    dve.wait_ge(ids_loaded[u], 16 * (TURNS * f + t + 1))
                    wait(dve, xg_loaded[u], 16 * (TURNS * f + t))
                    nc.vector.tensor_scalar(gather_ids[:, u:u + 1], slot_ids[:, bass.ds(b, 1)], 1, None,
                                            ALU.logical_shift_right).then_inc(gather_ids_done, 1)

                def tick(b, t, u):
                    par, last = u % 2, (u + 1) % 2
                    if is_block(b, -2):
                        to_gather(b + 2, t + (u + 2) // U, (u + 2) % U)
                    if is_block(b, 1):
                        v, tv = (u + U - 1) % U, t - (u == 0)
                        dve.wait_ge(hidT_in_psum, N + b)
                        wait(dve, y_in_psum, N + b - 2)
                        nc.vector.tensor_copy(flat(hidT[:, last]), bank[1][:, 0:D]).then_inc(hidT_ready, 1)
                        wait_apart(dve, (y_stored[v], 16 * (TURNS * f + tv)))
                        nc.vector.tensor_copy(scatter_ids[:, v:v + 1],
                                              slot_ids[:, bass.ds(b - 1, 1)]).then_inc(scatter_ids_done, 1)
                    if is_block(b, 0):
                        dve.wait_ge(act_g_done, N + b + 1)
                        nc.vector.tensor_tensor(hid[:, par], act_g[:, par], bank[2 + par][:, D:],
                                                ALU.mult).then_inc(hid_done, 1)

                for b in range(2):
                    to_gather(b, 0, b)
                run_blocks(dve, tick, 1, first=2)

            plan(0)
            keep(0)
            experts(0)
            phase_end(dve, 3)
            nc.vector.memset(e_sb[:, 1], 0.0).then_inc(e_zero, 1)

            def add_pairs(i, par, n):
                for r in range(R):
                    ins = nc.vector.scalar_tensor_tensor(
                        out=x_in[:, par, r, :], in0=pair_in[:, par, r, 0, :], scalar=weight[:, 0, r, bass.ds(i, 1)],
                        in1=x_in[:, par, r, :], op0=ALU.mult, op1=ALU.add)
                ins.then_inc(pair0_added, 1)
                dve.wait_ge(pair0_added, n + 1)
                for r in range(R):
                    ins = nc.vector.scalar_tensor_tensor(
                        out=x_in[:, par, r, :], in0=pair_in[:, par, r, 1, :], scalar=weight[:, 1, r, bass.ds(i, 1)],
                        in1=x_in[:, par, r, :], op0=ALU.mult, op1=ALU.add)
                return ins

            def ssm_input(i, t, par):
                if inside(i, 0):
                    dve.wait_ge(x_loaded[par], XL_SSM + 16 * (t + 1))
                    dve.wait_ge(pair_loaded[par], 16 * (t + 1))
                    add_pairs(i, par, i).then_inc(pair1_added, 1)
                    dve.wait_ge(pair1_added, i + 1)
                    layernorm(dve, LN_SSM + i, par)
                    normalize(dve, LN_SSM + i, par)
                if inside(i, 1):
                    dve.wait_ge(gelu_done, i)
                    dve.wait_ge(sig_done, i)
                    wait(dve, e_in_psum, i - 1)
                    nc.vector.tensor_tensor(flat(uT[:]), flat(gelu[:]), flat(sig[:]),
                                            ALU.mult).then_inc(uT_ready, 1)

            run_steps(dve, ssm_input, STEPS + 1)
            phase_end(dve, 4)

            for c in range(C):
                ins = nc.vector.tensor_copy(ends[:, c, :].rearrange("p (q r) -> p q r", r=R),
                                            e_sb[:, 1, c, :].rearrange("p (r q) -> p q r", r=R))
            ins.then_inc(ends_ready, 1)
            for k in range(LEVELS):
                width = CHUNKS - 2 ** k
                dve.wait_ge(ends_ready, k + 1)
                dve.wait_ge(level_in_psum, k + 1)
                for m in range(C):
                    later = ends[:, m, :].rearrange("p (b n) -> p b n", b=BATCHES)[:, :, 2 ** k:]
                    ins = nc.vector.tensor_tensor(
                        later, later, bank[6 + m][:, 0:BATCHES * width].rearrange("p (b n) -> p b n", b=BATCHES),
                        ALU.add)
                ins.then_inc(ends_ready, 1)
            dve.wait_ge(ends_ready, LEVELS + 1)
            per = P // BATCHES
            for c in range(C):
                nc.vector.tensor_copy(c_sb[:, 1, c, P:].rearrange("p (r q) -> p r q", r=R - 1),
                                      ends[:, c, :].rearrange("p (q r) -> p r q", r=R)[:, 0:R - 1, :])
                first = c_sb[:, 1, c, 0:P].rearrange("p (b q) -> p b q", b=BATCHES)
                nc.vector.tensor_copy(first[:, :, 1:],
                                      ends[:, c, :].rearrange("p (b q r) -> p b q r", b=BATCHES, r=R)[:, :, 0:per - 1, R - 1])
                ins = nc.vector.memset(first[:, :, 0:1], 0.0)
            ins.then_inc(carry_ready, 1)
            phase_end(dve, 5)

            def second_pass(i, t, par):
                last, tl = 1 - par, t - 1 + par
                if inside(i, 1):
                    dve.wait_ge(x_loaded[last], XL_SECOND + 16 * (tl + 1))
                    dve.wait_ge(ssm_in_psum, i)
                    for h in range(2):
                        x_h = flat(x_in[:, last, 2 * h:2 * h + 2])
                        ins = nc.vector.tensor_tensor(x_h, x_h, bank[6 + h][:], ALU.add)
                    ins.then_inc(x2_ready, 1)
                    dve.wait_ge(x2_ready, i)
                    layernorm(dve, LN_ROUTE[1] + i - 1, last)
                    if inside(i, 3):
                        dve.wait_ge(xn_stored[last], 8 * STEPS + 16 * tl)
                    normalize(dve, LN_ROUTE[1] + i - 1, last)
                if inside(i, 0):
                    dve.wait_ge(e_loaded[par], 16 * (t + 1))
                    dve.wait_ge(c_ready, i + 1)
                    nc.vector.tensor_tensor(flat(e_in[:, par]), flat(e_in[:, par]), flat(c_sb[:, par]),
                                            ALU.add).then_inc(s_ready, 1)
                if inside(i, 3):
                    route(1, i - 3, last)
                    send(1, i - 3, tl - 1, last)

            run_steps(dve, second_pass, STEPS + 3, first=4)
            phase_end(dve, 6)
            plan(1)
            keep(1)
            experts(1)
            phase_end(dve, 7)

            def last_pass(i, t, par):
                dve.wait_ge(x_loaded[par], XL_LAST + 16 * (t + 1))
                dve.wait_ge(pair_loaded[par], 8 * STEPS + 16 * (t + 1))
                add_pairs(i, par, STEPS + i).then_inc(out_ready, 1)

            run_steps(dve, last_pass)


_INS = ['L0_attn_x', 'L0_attn_W_u', 'L0_attn_b_u', 'L0_attn_W_g', 'L0_attn_b_g', 'L0_attn_A', 'L0_attn_Bm',
        'L0_attn_Cm', 'L0_attn_D', 'L0_ffn_router_w', 'L0_ffn_gate_w', 'L0_ffn_up_w', 'L0_ffn_down_w']
_OUTS = [((4, 2048, 256), 'float32')]


def kernel(**inputs):
    import numpy as _np
    import concourse.bacc as _bacc
    from concourse import mybir as _mybir
    from concourse.bass_utils import run_bass_kernel_spmd as _run

    nc = _bacc.Bacc("TRN2", target_bir_lowering=False, num_devices=1)
    arrays, args = {}, []
    for name in _INS:
        a = _np.ascontiguousarray(inputs[name])
        arrays[f"in_{name}_dram"] = a
        args.append(nc.dram_tensor(f"in_{name}_dram", a.shape, _mybir.dt.from_np(a.dtype), kind="ExternalInput").ap())
    for i, (shape, dtype) in enumerate(_OUTS):
        dt = _mybir.dt.from_np(_np.dtype(dtype))
        args.append(nc.dram_tensor(f"out_{i}_dram", shape, dt, kind="ExternalOutput").ap())
    macaron(nc, *args)
    r = _run(nc, [arrays], core_ids=[0])
    return r.results[0]["out_0_dram"]
```

```python
from contextlib import ExitStack

import concourse.bass as bass
from concourse import mybir

ALU = mybir.AluOpType
ACT = mybir.ActivationFunctionType
F32 = mybir.dt.float32
BF16 = mybir.dt.bfloat16
U32 = mybir.dt.uint32
X = mybir.AxisListType.X

P = 128
R = 4
STEPS = 16
D = 256
C = D // P
E = 16
K = 2
TOKENS = 4 * 2048
COLS = R * P
BATCHES = 4
CHUNKS = TOKENS // STEPS // BATCHES
CAPACITY = -(-TOKENS * K * 5 // (E * 4))
REGION = TOKENS
BLOCKS = TOKENS * K // P + E
SLOTS = E * REGION + E * P
NOBODY = 1 << 20
UNDERFLOW = -104.0
EPS = 1e-5
PLAN, KEEP = 5, 7
U = 8
G = U // 2
TURNS = BLOCKS // U
LAG = 5
LEVELS = CHUNKS.bit_length() - 1
SQUARES = LEVELS + STEPS.bit_length() - 2


def wait(eng, sem, value):
    if not isinstance(value, int) or value > 0:
        eng.wait_ge(sem, value)


def run_steps(eng, tick, total=STEPS, first=2, split=None, done=0):
    for i in range(done, first):
        tick(i, i // 2, i % 2)
    bounds = [first // 2] + ([split // 2] if split else []) + [STEPS // 2]
    for lo, hi in zip(bounds, bounds[1:]):
        with eng.Fori(lo, hi) as t:
            for par in range(2):
                if split:
                    tick(2 * t + par, t, par, hi == split // 2)
                else:
                    tick(2 * t + par, t, par)
    for i in range(STEPS, total):
        tick(i, i // 2, i % 2)


def inside(i, lag):
    return not isinstance(i, int) or 0 <= i - lag < STEPS


def run_blocks(eng, tick, extra, first=1):
    for b in range(U * first):
        tick(b, b // U, b % U)
    with eng.Fori(first, TURNS - 1) as t:
        for u in range(U):
            tick(U * t + u, t, u)
    for u in range(U + extra):
        tick(BLOCKS - U + u, TURNS - 1 + u // U, u % U)


def groups(t, u, ahead=0):
    g = u // G + ahead
    return g % 2, t + g // 2


def is_block(b, lag):
    return not isinstance(b, int) or 0 <= b - lag < BLOCKS


def macaron(nc, x, W_u, b_u, W_g, b_g, A, Bm, Cm, Dv, router_w, gate_w, up_w, down_w, out):
    x_v = x.rearrange("b (q r i) d -> i (b q) r d", r=R, i=STEPS)
    out_v = out.rearrange("b (q r i) d -> i (b q) r d", r=R, i=STEPS)

    def dram(name, shape, dt):
        return nc.dram_tensor(name, shape, dt, kind="Internal").ap()

    xn_d = [dram(f"xn_d{f}", [TOKENS, D], F32) for f in range(2)]
    pair_d = [dram(f"pair_d{f}", [TOKENS * K, D], F32) for f in range(2)]
    slot_d = [dram(f"slot_d{f}", [SLOTS, 1], U32) for f in range(2)]
    x1_d = dram("x1_d", [STEPS, P, R * D], F32)
    x2_d = dram("x2_d", [STEPS, P, R * D], F32)
    e_d = dram("e_d", [STEPS, P, C * COLS], F32)
    pow_d = dram("pow_d", [SQUARES, P, C * D], F32)
    xn_v = [t.rearrange("(i p r) d -> i p (r d)", p=P, r=R) for t in xn_d]
    pair_v = [t.rearrange("(i p q) d -> i p (q d)", p=P, q=R * K) for t in pair_d]

    with ExitStack() as ctx:
        def sb(name, shape, dt):
            return ctx.enter_context(nc.sbuf_tensor(name, shape, dt))

        def sem(name):
            return ctx.enter_context(nc.semaphore(name))

        def sems(name, n):
            return [sem(f"{name}{i}") for i in range(n)]

        w_gu = sb("w_gu", [P, C, E, 2 * D], F32)
        w_dn = sb("w_dn", [P, C, E, D], F32)
        r_w = sb("r_w", [P, C, E], F32)
        wT = {n: sb(f"wT_{n}", [P, C, D], F32) for n in ("u", "g", "b", "a", "c")}
        pw = sb("pw", [P, C, D], F32)
        pwT = sb("pwT", [P, C, D], F32)
        level_w = sb("level_w", [P, 2, C, D], F32)
        bias_u = sb("bias_u", [P, C], F32)
        bias_g = sb("bias_g", [P, C], F32)
        d_row = sb("d_row", [P, D], F32)
        ident = sb("ident", [P, P], F32)
        before = sb("before", [P, P], BF16)
        ones = sb("ones", [P, P], BF16)
        reset = sb("reset", [P, K * E, R * STEPS], BF16)
        iota_e = sb("iota_e", [P, E], U32)
        region0 = sb("region0", [P, E], F32)
        pair_no = sb("pair_no", [P, STEPS, R * K], U32)
        steps128 = sb("steps128", [E, REGION // P], F32)
        upto = sb("upto", [E, E], F32)
        ones_e = sb("ones_e", [E, 1], F32)
        block_no = sb("block_no", [E, BLOCKS], F32)
        block_row = sb("block_row", [1, BLOCKS], F32)
        minus_half = sb("minus_half", [P, R], F32)
        key = sb("key", [P, STEPS, R, E], F32)
        key2 = sb("key2", [P, STEPS, R], F32)
        chosen = sb("chosen", [P, K, E, R, STEPS], BF16)
        weight = sb("weight", [P, K, R, STEPS], F32)
        slot_ids = sb("slot_ids", [P, BLOCKS], U32)
        gather_ids = sb("gather_ids", [P, 2, G], U32)
        scatter_ids = sb("scatter_ids", [P, 2, G], U32)
        block_e = sb("block_e", [1, BLOCKS], U32)
        block_r = sb("block_r", [1, BLOCKS], U32)
        stats = sb("stats", [P, R, 6], F32)
        mv = sb("mv", [P, R, 2], F32)
        var = sb("var", [P, R], F32)
        rstd = sb("rstd", [P, R], F32)
        std = sb("std", [P, R], F32)
        guess = sb("guess", [P, R], F32)
        square = sb("square", [P, R], F32)
        shift = sb("shift", [P, R], F32)
        top = sb("top", [P, R], F32)
        key_cur = sb("key_cur", [P, R, E], F32)
        max8 = sb("max8", [P, R, 8], F32)
        idx8 = sb("idx8", [P, R, 8], U32)
        either = sb("either", [P, R, E], BF16)
        seen = sb("seen", [P, 2, E], BF16)
        added = sb("added", [P, E], F32)
        slot_e = sb("slot_e", [P, R, E], F32)
        slot_k = sb("slot_k", [P, R, K, E], F32)
        slot = sb("slot", [P, 2, R * K], U32)
        pair_cur = sb("pair_cur", [P, 2, R * K], U32)
        count_e = sb("count_e", [E, 1], F32)
        reached = sb("reached", [E, REGION // P], F32)
        blocks_e = sb("blocks_e", [E, 1], F32)
        ends_e = sb("ends_e", [E, 1], F32)
        skip_e = sb("skip_e", [E, 1], F32)
        past = sb("past", [E, BLOCKS], F32)
        incl = sb("incl", [P, K * E, R * STEPS], BF16)
        prefix = sb("prefix", [P, K * E], F32)
        exp2 = sb("exp2", [P, STEPS, R], F32)
        rden = sb("rden", [P, STEPS, R], F32)
        kept = sb("kept", [P, K, R * STEPS], F32)

        work = sb("work", [P, 15 * 1024], F32)

        def part(at, shape):
            n = 1
            for s in shape:
                n *= s
            names = "abcd"[:len(shape)]
            pat = f"p ({' '.join(names)}) -> p {' '.join(names)}"
            return work[:, at:at + n].rearrange(pat, **dict(zip(names, shape)))

        x_in = part(0, [2, R, D])
        pair_in = part(2048, [2, R, K, D])
        xn = part(6144, [2, R, D])
        xnT = part(8192, [C, COLS])
        gelu = part(9216, [C, COLS])
        sig = part(10240, [C, COLS])
        uT = part(12288, [C, COLS])
        e_sb = part(13312, [2, C, COLS])
        e_in = part(2048, [2, C, COLS])
        c_sb = part(4096, [2, C, COLS])
        ends = part(9216, [C, COLS])
        xg = part(9216, [U, D])
        y_sb = part(11264, [U, D])
        xgT = part(13312, [2, C, P])
        act_g = part(13824, [2, D])
        hid = part(14336, [2, D])
        hidT = part(14848, [2, C, P])
        rank = part(2048, [K * E, R * STEPS])
        exps = part(4096, [STEPS * R, E])
        raw = part(11264, [5, C, D])
        empty = part(9216, [1088]).bitcast(U32)

        bank = [ctx.enter_context(nc.psum_tensor(f"bank{i}", [P, 512], F32)) for i in range(8)]

        phase_done = sem("phase_done")
        const_step = sem("const_step")
        table_cleared = sem("table_cleared")
        empty_ready = sem("empty_ready")
        raw_loaded = sem("raw_loaded")
        small_loaded = sem("small_loaded")
        experts_loaded = sem("experts_loaded")
        router_loaded = sem("router_loaded")
        wT_in_psum = sem("wT_in_psum")
        wT_ready = sem("wT_ready")
        x_loaded = sems("x_loaded", 2)
        pair_loaded = sems("pair_loaded", 2)
        e_loaded = sems("e_loaded", 2)
        stats_done = sem("stats_done")
        mv_done = sem("mv_done")
        var_done = sem("var_done")
        rstd_done = sem("rstd_done")
        std_done = sem("std_done")
        guess_done = sem("guess_done")
        square_done = sem("square_done")
        ratio_done = sem("ratio_done")
        shift_done = sem("shift_done")
        xn_ready = sem("xn_ready")
        xn_stored = sems("xn_stored", 2)
        xnT_in_psum = sem("xnT_in_psum")
        xnT_ready = sem("xnT_ready")
        logits_done = sem("logits_done")
        top_done = sem("top_done")
        key_done = sem("key_done")
        key_clamped = sem("key_clamped")
        max8_done = sem("max8_done")
        idx8_done = sem("idx8_done")
        chosen_done = sem("chosen_done")
        either_done = sem("either_done")
        added_done = sem("added_done")
        seen_done = sem("seen_done")
        slots_in_psum = sem("slots_in_psum")
        slot_e_done = sem("slot_e_done")
        slot_k_done = sem("slot_k_done")
        slot_done = sem("slot_done")
        slot_written = sems("slot_written", 2)
        square_in_psum = sem("square_in_psum")
        square_ready = sem("square_ready")
        square_stored = sem("square_stored")
        plan_pe = sem("plan_pe")
        plan_dve = sem("plan_dve")
        keep_pe = sem("keep_pe")
        keep_act = sem("keep_act")
        keep_dve = sem("keep_dve")
        ids_loaded = sems("ids_loaded", 2)
        gather_ids_done = sem("gather_ids_done")
        scatter_ids_done = sem("scatter_ids_done")
        xg_loaded = sems("xg_loaded", U)
        xgT_in_psum = sem("xgT_in_psum")
        xgT_ready = sem("xgT_ready")
        gu_in_psum = sem("gu_in_psum")
        act_g_done = sem("act_g_done")
        hid_done = sem("hid_done")
        hidT_in_psum = sem("hidT_in_psum")
        hidT_ready = sem("hidT_ready")
        y_in_psum = sem("y_in_psum")
        y_ready = sem("y_ready")
        y_stored = sems("y_stored", 2)
        pair0_added = sem("pair0_added")
        pair1_added = sem("pair1_added")
        x1_ready = sem("x1_ready")
        x1_stored = sems("x1_stored", 2)
        ug_in_psum = sem("ug_in_psum")
        sig_done = sem("sig_done")
        gelu_done = sem("gelu_done")
        uT_ready = sem("uT_ready")
        e_zero = sem("e_zero")
        xg_zero = sem("xg_zero")
        e_in_psum = sem("e_in_psum")
        e_ready = sem("e_ready")
        e_stored = sems("e_stored", 2)
        ends_ready = sem("ends_ready")
        level_loaded = sems("level_loaded", 2)
        level_in_psum = sem("level_in_psum")
        carry_ready = sem("carry_ready")
        c_in_psum = sem("c_in_psum")
        c_ready = sem("c_ready")
        s_ready = sem("s_ready")
        ssm_in_psum = sem("ssm_in_psum")
        x2_ready = sem("x2_ready")
        x2_stored = sems("x2_stored", 2)
        out_ready = sem("out_ready")
        out_stored = sems("out_stored", 2)

        def phase_end(eng, k):
            eng.drain().then_inc(phase_done, 1)
            eng.wait_ge(phase_done, 5 * k)

        def wait_apart(eng, *waits):
            ready = [(sem, v if isinstance(v, int) else eng.compute_val(v)) for sem, v in waits
                     if not isinstance(v, int) or v > 0]
            eng.wait_ge(phase_done, 5)
            for sem, v in ready:
                eng.wait_ge(sem, v)

        LN_ROUTE, LN_SSM = (0, 2 * STEPS), STEPS
        XL_ROUTE, XL_SSM, XL_SECOND, XL_LAST = (16 * n * STEPS // 2 for n in range(4))

        def layernorm(dve, n, par):
            for r in range(R):
                ins = nc.vector.bn_stats(stats[:, r, :], x_in[:, par, r, :])
            ins.then_inc(stats_done, 1)
            wait_apart(dve, (stats_done, n + 1))
            for r in range(R):
                ins = nc.vector.bn_aggr(mv[:, r, :], stats[:, r, :])
            ins.then_inc(mv_done, 1)
            dve.wait_ge(mv_done, n + 1)
            wait(dve, rstd_done, n)
            nc.vector.tensor_scalar(var[:], mv[:, :, 1], EPS, None, ALU.add).then_inc(var_done, 1)
            wait(dve, xnT_in_psum, n - 1)
            dve.wait_ge(rstd_done, n + 1)

        def normalize(dve, n, par):
            for r in range(R):
                ins = nc.vector.tensor_scalar(xn[:, par, r, :], x_in[:, par, r, :], mv[:, r, 0:1],
                                              rstd[:, r:r + 1], ALU.subtract, ALU.mult)
            ins.then_inc(xn_ready, 1)

        def rstd_step(pool, n):
            pool.wait_ge(var_done, n + 1)
            wait(pool, xn_ready, n)
            nc.gpsimd.tensor_tensor(rstd[:], var[:], minus_half[:], ALU.pow).then_inc(rstd_done, 1)

        def turn_xn(pe, n, par):
            pe.wait_ge(xn_ready, n + 1)
            wait(pe, xnT_ready, n)
            for c in range(C):
                for r in range(R):
                    ins = nc.tensor.transpose(bank[c][:, r * P:(r + 1) * P],
                                              xn[:, par, r, c * P:(c + 1) * P], ident[:])
            ins.then_inc(xnT_in_psum, 1)

        def copy_xnT(act, n, users, used):
            act.wait_ge(xnT_in_psum, n + 1)
            wait(act, users, used)
            for c in range(C):
                ins = nc.scalar.copy(xnT[:, c, :], bank[c][:])
            ins.then_inc(xnT_ready, 1)

        def flat(ap):
            names = "abcd"[:len(ap.shape) - 1]
            return ap.rearrange(f"p {' '.join(names)} -> p ({' '.join(names)})")

        block = ctx.enter_context(nc.Block())

        @block.sync
        def _(sp):
            def load_x(i, t, par):
                wait(sp, xn_ready, i - 1)
                sp.dma_start(x_in[:, par], x_v[i]).then_inc(x_loaded[par], 16)

            load_x(0, 0, 0)
            for n, w in enumerate((W_u, W_g, Bm, A, Cm)):
                sp.dma_start(raw[:, n], w.rearrange("(c p) d -> p c d", p=P)).then_inc(raw_loaded, 16)
            sp.dma_start(pw[:], A.rearrange("(c p) d -> p c d", p=P)).then_inc(raw_loaded, 16)
            load_x(1, 0, 1)
            sp.dma_start(r_w[:], router_w.rearrange("(c p) e -> p c e", p=P)).then_inc(router_loaded, 16)
            for dst, b in ((bias_u, b_u), (bias_g, b_g)):
                for c in range(C):
                    sp.dma_start(dst[:, c:c + 1],
                                 b.rearrange("(c p a) -> c p a", p=P, a=1)[c]).then_inc(small_loaded, 16)
            sp.dma_start(d_row[:], Dv.rearrange("(a d) -> a d", a=1).broadcast_to([P, D])).then_inc(small_loaded, 16)
            sp.wait_ge(empty_ready, 1)
            for f in range(2):
                sp.dma_start(slot_d[f].rearrange("(p s) a -> p (s a)", p=P),
                             empty[:, 0:SLOTS // P]).then_inc(table_cleared, 16)
            phase_end(sp, 1)

            def load_route(i, t, par):
                if inside(i, 2):
                    load_x(i, t, par)
                for dst, w in ((w_gu[:, :, i, 0:D], gate_w), (w_gu[:, :, i, D:], up_w), (w_dn[:, :, i, :], down_w)):
                    sp.dma_start(dst, w[i].rearrange("(c p) h -> p c h", p=P)).then_inc(experts_loaded, 16)

            run_steps(sp, load_route)
            phase_end(sp, 2)

            def load_ids(f):
                def load(b, t, u):
                    par, n = groups(t, u)
                    if u % G == 0 and (f or not isinstance(b, int) or b >= U):
                        wait_apart(sp, (ids_loaded[par], 16 * G * (f * TURNS + n)))
                    row = sp.value_load(block_r[0:1, bass.ds(b, 1)], min_val=0, max_val=SLOTS - P)
                    sp.dma_start(slot_ids[:, bass.ds(b, 1)],
                                 slot_d[f][bass.ds(row, P), :]).then_inc(ids_loaded[par], 16)

                run_blocks(sp, load, 0)

            load_ids(0)
            for par in range(2):
                sp.dma_start(x_in[:, par], x_v[par]).then_inc(x_loaded[par], 16)
            phase_end(sp, 3)

            def load_ssm(i, t, par):
                if inside(i, 2):
                    wait(sp, x1_stored[par], 16 * t)
                    sp.dma_start(x_in[:, par], x_v[i]).then_inc(x_loaded[par], 16)
                wait(sp, pair1_added, i - 1)
                sp.dma_start(flat(pair_in[:, par]), pair_v[0][i]).then_inc(pair_loaded[par], 16)

            run_steps(sp, load_ssm)
            phase_end(sp, 4)
            for k in range(LEVELS):
                wait(sp, level_in_psum, k - 1)
                sp.dma_start(flat(level_w[:, k % 2]), pow_d[SQUARES - LEVELS + k]).then_inc(level_loaded[k % 2], 16)
            phase_end(sp, 5)

            def second_pass(i, t, par):
                if inside(i, 2):
                    sp.wait_ge(x2_ready, i - 1)
                    sp.dma_start(x2_d[i - 2], flat(x_in[:, par])).then_inc(x2_stored[par], 16)
                if inside(i, 0):
                    wait(sp, ssm_in_psum, i - 1)
                    sp.dma_start(flat(e_in[:, par]), e_d[i]).then_inc(e_loaded[par], 16)
                    if inside(i, 2):
                        wait_apart(sp, (x2_stored[par], 16 * t),
                                   (xn_ready, LN_ROUTE[1] + i - 1))
                    sp.dma_start(flat(x_in[:, par]), x1_d[i]).then_inc(x_loaded[par], 16)

            run_steps(sp, second_pass, STEPS + 2)
            for par in range(2):
                sp.wait_ge(x2_stored[par], 8 * STEPS)
            phase_end(sp, 6)
            load_ids(1)
            for par in range(2):
                sp.dma_start(flat(x_in[:, par]), x2_d[par]).then_inc(x_loaded[par], 16)
            phase_end(sp, 7)

            def last_pass(i, t, par):
                if inside(i, 2):
                    sp.wait_ge(out_ready, i - 1)
                    sp.dma_start(out_v[i - 2], x_in[:, par]).then_inc(out_stored[par], 16)
                if inside(i, 0):
                    sp.dma_start(flat(pair_in[:, par]), pair_v[1][i]).then_inc(pair_loaded[par], 16)
                    if inside(i, 2):
                        sp.wait_ge(out_stored[par], 16 * t)
                        sp.dma_start(flat(x_in[:, par]), x2_d[i]).then_inc(x_loaded[par], 16)

            run_steps(sp, last_pass, STEPS + 2)
            for par in range(2):
                sp.wait_ge(out_stored[par], 8 * STEPS)

        @block.gpsimd
        def _(pool):
            nc.gpsimd.memset(empty[:], NOBODY).then_inc(empty_ready, 1)
            nc.gpsimd.memset(ident[:], 0.0)
            nc.gpsimd.memset(ones[:], 1.0)
            nc.gpsimd.memset(upto[:], 1.0)
            nc.gpsimd.memset(ones_e[:], 1.0)
            nc.gpsimd.memset(minus_half[:], -0.5)
            nc.gpsimd.memset(seen[:, 0], 0.0)
            nc.gpsimd.memset(before[:], 1.0)
            nc.gpsimd.memset(reset[:], 1.0).then_inc(const_step, 1)
            pool.wait_ge(const_step, 1)
            nc.gpsimd.affine_select(out=ident[:], in_=ident[:], compare_op=ALU.not_equal, fill=1.0,
                                    base=0, pattern=[[-1, P]], channel_multiplier=1)
            nc.gpsimd.affine_select(out=before[:], in_=before[:], compare_op=ALU.is_gt, fill=0.0,
                                    base=0, pattern=[[1, P]], channel_multiplier=-1)
            nc.gpsimd.affine_select(out=upto[:], in_=upto[:], compare_op=ALU.is_ge, fill=0.0,
                                    base=0, pattern=[[1, E]], channel_multiplier=-1)
            nc.gpsimd.memset(reset[:, :, 0:1], 0.0)
            nc.gpsimd.iota(iota_e[:], pattern=[[1, E]], base=0, channel_multiplier=0)
            nc.gpsimd.iota(region0[:], pattern=[[REGION, E]], base=0, channel_multiplier=0,
                           allow_small_or_imprecise_dtypes=True)
            nc.gpsimd.iota(pair_no[:], pattern=[[COLS * K, STEPS], [1, R * K]], base=0,
                           channel_multiplier=R * K)
            nc.gpsimd.iota(steps128[:], pattern=[[P, REGION // P]], base=0, channel_multiplier=0,
                           allow_small_or_imprecise_dtypes=True)
            nc.gpsimd.iota(block_no[:], pattern=[[1, BLOCKS]], base=0, channel_multiplier=0,
                           allow_small_or_imprecise_dtypes=True)
            nc.gpsimd.iota(block_row[:], pattern=[[P, BLOCKS]], base=0, channel_multiplier=0,
                           allow_small_or_imprecise_dtypes=True)
            phase_end(pool, 1)

            def write_slots(f, i, par):
                wait_apart(pool, (slot_done, STEPS * f + i + 1))
                for q in range(R * K):
                    nc.gpsimd.indirect_dma_start(
                        out=slot_d[f], out_offset=bass.IndirectOffsetOnAxis(ap=slot[:, par, q:q + 1], axis=0),
                        in_=pair_cur[:, par, q:q + 1], in_offset=None).then_inc(slot_written[par], 16)

            def clear_xg(f):
                nc.gpsimd.memset(xg[:], 0.0).then_inc(xg_zero, 1)
                pool.wait_ge(xg_zero, f + 1)

            def all_written(f):
                for par in range(2):
                    pool.wait_ge(slot_written[par], 16 * R * K * (STEPS // 2) * (f + 1))

            pool.wait_ge(table_cleared, 32)
            run_steps(pool, lambda i, t, par: write_slots(0, i, par))
            clear_xg(0)
            all_written(0)
            phase_end(pool, 2)

            def experts(f):
                def tick(b, t, u):
                    n = BLOCKS * f + b
                    if is_block(b, 0):
                        if u % G == 0:
                            wait_apart(pool, (gather_ids_done, 2 * TURNS * f + 2 * t + u // G + 1))
                        wait_apart(pool, (xgT_in_psum, n - U + 1))
                        nc.gpsimd.indirect_dma_start(
                            out=xg[:, u], out_offset=None, in_=xn_d[f],
                            in_offset=bass.IndirectOffsetOnAxis(ap=gather_ids[:, u // G, u % G:u % G + 1], axis=0),
                            bounds_check=TOKENS - 1, oob_is_err=False).then_inc(xg_loaded[u], 16)
                    if is_block(b, LAG):
                        v, tv = (u - LAG) % U, t - (u < LAG)
                        if v % G == 0:
                            wait_apart(pool, (scatter_ids_done, 2 * TURNS * f + 2 * tv + v // G + 1))
                        wait_apart(pool, (y_ready, n - LAG + 1))
                        nc.gpsimd.indirect_dma_start(
                            out=pair_d[f],
                            out_offset=bass.IndirectOffsetOnAxis(ap=scatter_ids[:, v // G, v % G:v % G + 1], axis=0),
                            in_=y_sb[:, v], in_offset=None,
                            bounds_check=TOKENS * K - 1, oob_is_err=False).then_inc(y_stored[v // G], 16)

                run_blocks(pool, tick, LAG)
                for h in range(2):
                    pool.wait_ge(y_stored[h], 16 * G * TURNS * (f + 1))

            experts(0)
            phase_end(pool, 3)

            def ssm_input(i, t, par):
                rstd_step(pool, LN_SSM + i)
                pool.wait_ge(xn_ready, LN_SSM + i + 1)
                nc.gpsimd.tensor_tensor(x_in[:, par], x_in[:, par],
                                        d_row[:].unsqueeze(1).broadcast_to([P, R, D]),
                                        ALU.add).then_inc(x1_ready, 1)
                wait_apart(pool, (x1_ready, i + 1))
                pool.dma_start(x1_d[i], flat(x_in[:, par])).then_inc(x1_stored[par], 16)

            run_steps(pool, ssm_input)
            for par in range(2):
                pool.wait_ge(x1_stored[par], 8 * STEPS)
            phase_end(pool, 4)
            phase_end(pool, 5)

            run_steps(pool, lambda i, t, par: write_slots(1, i, par))
            clear_xg(1)
            all_written(1)
            phase_end(pool, 6)
            experts(1)
            phase_end(pool, 7)

        @block.scalar
        def _(act):
            act.wait_ge(small_loaded, 80)
            phase_end(act, 1)
            for n, name in enumerate("ugbac"):
                act.wait_ge(wT_in_psum, n + 1)
                nc.scalar.copy(flat(wT[name][:]), bank[n][:]).then_inc(wT_ready, 1)
            nc.scalar.copy(flat(pwT[:]), bank[3][:]).then_inc(wT_ready, 1)

            def root(f, i):
                act.wait_ge(var_done, LN_ROUTE[f] + i + 1)
                nc.scalar.activation(std[:], var[:], ACT.Sqrt).then_inc(std_done, 1)

            def normalize_and_store(f, i, t, par):
                n = LN_ROUTE[f] + i
                act.wait_ge(shift_done, STEPS * f + i + 1)
                wait(act, xnT_in_psum, n - 1)
                if inside(i, 2):
                    act.wait_ge(xn_stored[par], 8 * STEPS * f + 16 * t)
                for r in range(R):
                    ins = nc.scalar.activation(xn[:, par, r, :], x_in[:, par, r, :], ACT.Identity,
                                               bias=shift[:, r:r + 1], scale=rstd[:, r:r + 1])
                ins.then_inc(xn_ready, 1)
                act.wait_ge(xn_ready, n + 1)
                act.dma_start(xn_v[f][i], flat(xn[:, par])).then_inc(xn_stored[par], 16)

            def copy_square(i):
                act.wait_ge(square_in_psum, i + 1)
                wait(act, square_stored, 16 * i)
                nc.scalar.copy(flat(pw[:]), bank[4][:])
                nc.scalar.copy(flat(pwT[:]), bank[5][:]).then_inc(square_ready, 1)
                act.wait_ge(square_ready, i + 1)
                act.dma_start(pow_d[i], flat(pwT[:])).then_inc(square_stored, 16)

            def route0(i, t, par, squares=True):
                root(0, i)
                normalize_and_store(0, i, t, par)
                if squares and inside(i, 1):
                    copy_square(i - 1)
                copy_xnT(act, LN_ROUTE[0] + i, logits_done, i)
            run_steps(act, route0, split=SQUARES)
            copy_square(SQUARES - 1)
            act.wait_ge(square_stored, 16 * SQUARES)
            for par in range(2):
                act.wait_ge(xn_stored[par], 8 * STEPS)
            phase_end(act, 2)

            def experts(f):
                N = BLOCKS * f
                nc.scalar.activation(exps[:], key[:].rearrange("p i r e -> p (i r) e"), ACT.Exp)
                nc.scalar.activation(exp2[:], key2[:], ACT.Exp).then_inc(keep_act, 1)

                def copy_xgT(b, par):
                    act.wait_ge(xgT_in_psum, N + b + 1)
                    wait(act, gu_in_psum, N + b - 1)
                    nc.scalar.copy(flat(xgT[:, par]), bank[0][:, 0:D]).then_inc(xgT_ready, 1)

                def tick(b, t, u):
                    if is_block(b, -1):
                        copy_xgT(b + 1, (u + 1) % 2)
                    if is_block(b, 0):
                        act.wait_ge(gu_in_psum, N + b + 1)
                        wait(act, hid_done, N + b - 1)
                        nc.scalar.activation(act_g[:, u % 2], bank[2 + u % 2][:, 0:D],
                                             ACT.Silu).then_inc(act_g_done, 1)
                    if is_block(b, 1):
                        v, tv = (u - 1) % U, t - (u == 0)
                        if v % G == 0:
                            wait(act, y_stored[v // G], 16 * G * (TURNS * f + tv))
                        act.wait_ge(y_in_psum, N + b)
                        nc.scalar.copy(y_sb[:, v], bank[4 + v % 2][:, 0:D]).then_inc(y_ready, 1)

                copy_xgT(0, 0)
                run_blocks(act, tick, 1)

            experts(0)
            phase_end(act, 3)

            def ssm_input(i, t, par):
                if inside(i, 1):
                    act.wait_ge(ug_in_psum, i)
                    wait(act, uT_ready, i - 1)
                    for m in range(C):
                        ins = nc.scalar.activation(gelu[:, m, :], bank[2 + m][:], ACT.Gelu,
                                                   bias=bias_u[:, m:m + 1])
                    ins.then_inc(gelu_done, 1)
                    for m in range(C):
                        ins = nc.scalar.activation(sig[:, m, :], bank[4 + m][:], ACT.Sigmoid,
                                                   bias=bias_g[:, m:m + 1])
                    ins.then_inc(sig_done, 1)
                if inside(i, 0):
                    copy_xnT(act, LN_SSM + i, ug_in_psum, i)
                if inside(i, 2):
                    act.wait_ge(e_in_psum, i - 1)
                    wait(act, e_stored[par], 16 * (t - 1))
                    for m in range(C):
                        ins = nc.scalar.copy(e_sb[:, par, m, :], bank[6 + m][:])
                    ins.then_inc(e_ready, 1)
                    act.wait_ge(e_ready, i - 1)
                    act.dma_start(e_d[i - 2], flat(e_sb[:, par])).then_inc(e_stored[par], 16)

            run_steps(act, ssm_input, STEPS + 2, first=4)
            for par in range(2):
                act.wait_ge(e_stored[par], 8 * STEPS)
            phase_end(act, 4)
            phase_end(act, 5)

            def second_pass(i, t, par):
                if inside(i, 2):
                    normalize_and_store(1, i - 2, t - 1, par)
                if inside(i, 0):
                    act.wait_ge(c_in_psum, i + 1)
                    wait(act, s_ready, i - 1)
                    for m in range(C):
                        ins = nc.scalar.copy(c_sb[:, par, m, :], bank[4 + m][:])
                    ins.then_inc(c_ready, 1)
                if inside(i, 2):
                    copy_xnT(act, LN_ROUTE[1] + i - 2, logits_done, STEPS + i - 2)
                if inside(i, 1):
                    root(1, i - 1)

            run_steps(act, second_pass, STEPS + 2, first=4)
            for par in range(2):
                act.wait_ge(xn_stored[par], 16 * STEPS)
            phase_end(act, 6)
            experts(1)
            phase_end(act, 7)

        @block.tensor
        def _(pe):
            pe.wait_ge(raw_loaded, 96)
            phase_end(pe, 1)
            for n in range(5):
                for k in range(C):
                    for m in range(C):
                        ins = nc.tensor.transpose(bank[n][:, k * D + m * P:k * D + (m + 1) * P],
                                                  raw[:, n, m, k * P:(k + 1) * P], ident[:])
                ins.then_inc(wT_in_psum, 1)
            pe.wait_ge(wT_ready, 6)
            pe.wait_ge(router_loaded, 16)

            def product(out_of, lhs, rhs, m_range=range(C)):
                for m in m_range:
                    for c in range(C):
                        ins = nc.tensor.matmul(out_of(m), lhs(c, m), rhs(c), start=(c == 0), stop=(c == C - 1))
                return ins

            def route_logits(f, i):
                pe.wait_ge(xnT_ready, LN_ROUTE[f] + i + 1)
                wait(pe, key_done, STEPS * f + i)
                for r in range(R):
                    for c in range(C):
                        ins = nc.tensor.matmul(bank[2][:, r * E:(r + 1) * E], xnT[:, c, r * P:(r + 1) * P],
                                               r_w[:, c, :], start=(c == 0), stop=(c == C - 1))
                ins.then_inc(logits_done, 1)

            def route_slots(f, i, par):
                n = STEPS * f + i
                pe.wait_ge(either_done, n + 1)
                wait(pe, seen_done, n)
                wait(pe, slot_e_done, n)
                place = bank[3][:, 0:R * E].rearrange("p (r e) -> p r e", r=R)
                nc.tensor.matmul(place, before[:], either[:], start=True, stop=False)
                for r in range(R - 1):
                    nc.tensor.matmul(place[:, r + 1:, :], ones[:],
                                     either[:, r:r + 1, :].broadcast_to([P, R - 1 - r, E]),
                                     start=False, stop=False)
                nc.tensor.matmul(place, ones[:], seen[:, par].unsqueeze(1).broadcast_to([P, R, E]),
                                 start=False, stop=True).then_inc(slots_in_psum, 1)

            def route0(i, t, par, squares=True):
                if inside(i, 0):
                    turn_xn(pe, LN_ROUTE[0] + i, par)
                    if squares:
                        wait(pe, square_ready, i)
                        product(lambda m: bank[4][:, m * D:(m + 1) * D],
                                lambda c, m: pwT[:, c, m * P:(m + 1) * P], lambda c: pw[:, c, :])
                        product(lambda m: bank[5][:, m * D:(m + 1) * D],
                                lambda c, m: pw[:, c, m * P:(m + 1) * P],
                                lambda c: pwT[:, c, :]).then_inc(square_in_psum, 1)
                    route_logits(0, i)
                if inside(i, 1):
                    route_slots(0, i - 1, 1 - par)

            run_steps(pe, route0, STEPS + 1, split=SQUARES)

            def plan(f):
                at = PLAN * f
                pe.wait_ge(seen_done, STEPS * (f + 1))
                pe.wait_ge(slot_e_done, STEPS * (f + 1))
                nc.tensor.matmul(bank[2][0:E, 0:1], seen[:, 0], ones[:, 0:1], start=True,
                                 stop=True).then_inc(plan_pe, 1)
                pe.wait_ge(plan_dve, at + 2)
                nc.tensor.matmul(bank[3][0:E, 0:1], upto[:], blocks_e[:], start=True,
                                 stop=True).then_inc(plan_pe, 1)
                pe.wait_ge(plan_dve, at + 4)
                nc.tensor.matmul(bank[2][0:1, 0:BLOCKS], ones_e[:], past[:], start=True, stop=True)
                nc.tensor.matmul(bank[3][0:1, 0:BLOCKS], skip_e[:], past[:], start=True,
                                 stop=True).then_inc(plan_pe, 1)

            def experts(f):
                N = BLOCKS * f
                pe.wait_ge(experts_loaded, 16 * 3 * E)

                def turn_xg(b, t, u):
                    pe.wait_ge(xg_loaded[u], 16 * (TURNS * f + t + 1))
                    wait(pe, xgT_ready, N + b)
                    for c in range(C):
                        ins = nc.tensor.transpose(bank[0][:, c * P:(c + 1) * P], xg[:, u, c * P:(c + 1) * P], ident[:])
                    ins.then_inc(xgT_in_psum, 1)

                def tick(b, t, u):
                    par, last = u % 2, (u + 1) % 2
                    if is_block(b, 0):
                        e = pe.value_load(block_e[0:1, bass.ds(b, 1)], min_val=0, max_val=E - 1)
                        pe.wait_ge(xgT_ready, N + b + 1)
                        wait(pe, hid_done, N + b - 1)
                        nc.tensor.matmul(bank[2 + par][:], xgT[:, par, 0, :], w_gu[:, 0, e, :],
                                         start=True, stop=False)
                    if is_block(b, 1):
                        pe.wait_ge(hid_done, N + b)
                        wait(pe, hidT_ready, N + b - 1)
                        for c in range(C):
                            ins = nc.tensor.transpose(bank[1][:, c * P:(c + 1) * P],
                                                      hid[:, last, c * P:(c + 1) * P], ident[:])
                        ins.then_inc(hidT_in_psum, 1)
                    if is_block(b, -1):
                        turn_xg(b + 1, t + (u + 1) // U, (u + 1) % U)
                    if is_block(b, 0):
                        nc.tensor.matmul(bank[2 + par][:], xgT[:, par, 1, :], w_gu[:, 1, e, :],
                                         start=False, stop=True).then_inc(gu_in_psum, 1)
                    if is_block(b, 1):
                        e = pe.value_load(block_e[0:1, bass.ds(b - 1, 1)], min_val=0, max_val=E - 1)
                        pe.wait_ge(hidT_ready, N + b)
                        wait(pe, y_ready, N + b - 2)
                        for c in range(C):
                            ins = nc.tensor.matmul(bank[4 + last][:, 0:D], hidT[:, last, c, :], w_dn[:, c, e, :],
                                                   start=(c == 0), stop=(c == C - 1))
                        ins.then_inc(y_in_psum, 1)

                    if isinstance(b, int) and b == 1:
                        pe.wait_ge(keep_dve, KEEP * f + 1)
                        nc.tensor.matmul(bank[6][:, 0:K * E], before[:], incl[:, :, R * STEPS - 1], start=True,
                                         stop=True).then_inc(keep_pe, 1)

                turn_xg(0, 0, 0)
                run_blocks(pe, tick, 1)

            plan(0)
            phase_end(pe, 2)
            experts(0)
            phase_end(pe, 3)
            pe.wait_ge(e_zero, 1)

            def weight_of(name):
                return lambda c, m: wT[name][:, c, m * P:(m + 1) * P]

            def ssm_input(i, t, par):
                if inside(i, 1):
                    pe.wait_ge(xnT_ready, LN_SSM + i)
                    wait(pe, gelu_done, i - 1)
                    wait(pe, sig_done, i - 1)
                    product(lambda m: bank[2 + m][:], weight_of("u"), lambda c: xnT[:, c, :])
                    product(lambda m: bank[4 + m][:], weight_of("g"),
                            lambda c: xnT[:, c, :]).then_inc(ug_in_psum, 1)
                if inside(i, 0):
                    turn_xn(pe, LN_SSM + i, par)
                if inside(i, 2):
                    pe.wait_ge(uT_ready, i - 1)
                    wait(pe, e_ready, i - 2)
                    for m in range(C):
                        for c in range(C):
                            nc.tensor.matmul(bank[6 + m][:], weight_of("b")(c, m), uT[:, c, :],
                                             start=(c == 0), stop=False)
                        for c in range(C):
                            ins = nc.tensor.matmul(bank[6 + m][:], weight_of("a")(c, m), e_sb[:, 1 - par, c, :],
                                                   start=False, stop=(c == C - 1))
                    ins.then_inc(e_in_psum, 1)

            run_steps(pe, ssm_input, STEPS + 2, first=4)
            phase_end(pe, 4)
            for k in range(LEVELS):
                width = CHUNKS - 2 ** k
                pe.wait_ge(ends_ready, k + 1)
                pe.wait_ge(level_loaded[k % 2], 16 * (k // 2 + 1))
                for m in range(C):
                    for c in range(C):
                        ins = nc.tensor.matmul(
                            bank[6 + m][:, 0:BATCHES * width].rearrange("p (b n) -> p b n", b=BATCHES),
                            level_w[:, k % 2, c, m * P:(m + 1) * P],
                            ends[:, c, :].rearrange("p (b n) -> p b n", b=BATCHES)[:, :, 0:width],
                            start=(c == 0), stop=(c == C - 1))
                ins.then_inc(level_in_psum, 1)
            phase_end(pe, 5)
            pe.wait_ge(carry_ready, 1)

            def second_pass(i, t, par):
                last = 1 - par
                if inside(i, 0):
                    wait(pe, c_ready, i)
                    product(lambda m: bank[4 + m][:], weight_of("a"),
                            lambda c: c_sb[:, last, c, :]).then_inc(c_in_psum, 1)
                if inside(i, 2):
                    turn_xn(pe, LN_ROUTE[1] + i - 2, par)
                if inside(i, 1):
                    pe.wait_ge(s_ready, i)
                    wait(pe, x2_ready, i - 1)
                    for r in range(R):
                        for c in range(C):
                            ins = nc.tensor.matmul(bank[6 + r // 2][:, (r % 2) * D:(r % 2 + 1) * D],
                                                   e_in[:, last, c, r * P:(r + 1) * P], wT["c"][:, c, :],
                                                   start=(c == 0), stop=(c == C - 1))
                    ins.then_inc(ssm_in_psum, 1)
                if inside(i, 2):
                    route_logits(1, i - 2)
                if inside(i, 3):
                    route_slots(1, i - 3, last)

            run_steps(pe, second_pass, STEPS + 3, first=4)
            plan(1)
            phase_end(pe, 6)
            experts(1)
            phase_end(pe, 7)

        @block.vector
        def _(dve):
            phase_end(dve, 1)

            def norm(f, i, par):
                n, k = LN_ROUTE[f] + i, STEPS * f + i
                for r in range(R):
                    ins = nc.vector.bn_stats(stats[:, r, :], x_in[:, par, r, :])
                ins.then_inc(stats_done, 1)
                wait_apart(dve, (stats_done, n + 1))
                for r in range(R):
                    ins = nc.vector.bn_aggr(mv[:, r, :], stats[:, r, :])
                ins.then_inc(mv_done, 1)
                dve.wait_ge(mv_done, n + 1)
                nc.vector.tensor_scalar(var[:], mv[:, :, 1], EPS, None, ALU.add).then_inc(var_done, 1)
                dve.wait_ge(std_done, k + 1)
                nc.vector.reciprocal(guess[:], std[:]).then_inc(guess_done, 1)
                dve.wait_ge(guess_done, k + 1)
                nc.vector.tensor_tensor(square[:], guess[:], guess[:], ALU.mult).then_inc(square_done, 1)
                dve.wait_ge(square_done, k + 1)
                nc.vector.scalar_tensor_tensor(out=square[:], in0=square[:], scalar=-0.5, in1=var[:],
                                               op0=ALU.mult, op1=ALU.mult).then_inc(ratio_done, 1)
                wait(dve, xn_ready, n)
                dve.wait_ge(ratio_done, k + 1)
                nc.vector.scalar_tensor_tensor(out=rstd[:], in0=square[:], scalar=1.5, in1=guess[:],
                                               op0=ALU.add, op1=ALU.mult).then_inc(rstd_done, 1)
                dve.wait_ge(rstd_done, n + 1)
                nc.vector.scalar_tensor_tensor(out=shift[:], in0=mv[:, :, 0], scalar=-1.0, in1=rstd[:],
                                               op0=ALU.mult, op1=ALU.mult).then_inc(shift_done, 1)

            def choose(f, i, par):
                m = STEPS * f + i
                lg = bank[2][:, 0:R * E].rearrange("p (r e) -> p r e", r=R)
                dve.wait_ge(logits_done, m + 1)
                nc.vector.tensor_reduce(top[:], lg, X, ALU.max).then_inc(top_done, 1)
                dve.wait_ge(top_done, m + 1)
                nc.vector.tensor_tensor(key_cur[:], lg, top[:].unsqueeze(2).broadcast_to([P, R, E]),
                                        ALU.subtract).then_inc(key_done, 1)
                dve.wait_ge(key_done, m + 1)
                nc.vector.tensor_scalar(key_cur[:], key_cur[:], UNDERFLOW, None, ALU.max).then_inc(key_clamped, 1)
                wait_apart(dve, (key_clamped, m + 1))
                for r in range(R):
                    ins = nc.vector.max(max8[:, r, :], key_cur[:, r, :])
                ins.then_inc(max8_done, 1)
                nc.vector.tensor_copy(key[:, i], key_cur[:])
                wait_apart(dve, (max8_done, m + 1))
                for r in range(R):
                    ins = nc.vector.max_index(idx8[:, r, :], max8[:, r, :], key_cur[:, r, :])
                ins.then_inc(idx8_done, 1)
                nc.vector.tensor_copy(key2[:, i], max8[:, :, 1])
                dve.wait_ge(idx8_done, m + 1)
                nc.vector.tensor_tensor(
                    chosen[:, :, :, :, i].rearrange("p k e r -> p k r e"),
                    idx8[:, :, 0:K].rearrange("p r k -> p k r").unsqueeze(3).broadcast_to([P, K, R, E]),
                    iota_e[:].unsqueeze(1).unsqueeze(1).broadcast_to([P, K, R, E]), ALU.is_equal).then_inc(chosen_done, 1)
                dve.wait_ge(chosen_done, m + 1)
                wait(dve, slots_in_psum, m)
                nc.vector.tensor_tensor(either[:], chosen[:, 0, :, :, i].rearrange("p e r -> p r e"),
                                        chosen[:, 1, :, :, i].rearrange("p e r -> p r e"),
                                        ALU.add).then_inc(either_done, 1)
                dve.wait_ge(either_done, m + 1)
                nc.vector.tensor_reduce(added[:], either[:].rearrange("p r e -> p e r"), X,
                                        ALU.add).then_inc(added_done, 1)
                dve.wait_ge(added_done, m + 1)
                nc.vector.tensor_tensor(seen[:, 1 - par], seen[:, par], added[:], ALU.add).then_inc(seen_done, 1)

            def place(f, i, t, par):
                m = STEPS * f + i
                wait_apart(dve, (slot_written[par], 16 * R * K * (STEPS // 2 * f + t)))
                nc.vector.tensor_copy(pair_cur[:, par], pair_no[:, i])
                dve.wait_ge(slots_in_psum, m + 1)
                nc.vector.tensor_tensor(slot_e[:], bank[3][:, 0:R * E].rearrange("p (r e) -> p r e", r=R),
                                        region0[:].unsqueeze(1).broadcast_to([P, R, E]),
                                        ALU.add).then_inc(slot_e_done, 1)
                dve.wait_ge(slot_e_done, m + 1)
                nc.vector.tensor_tensor(slot_k[:], chosen[:, :, :, :, i].rearrange("p k e r -> p r k e"),
                                        slot_e[:].unsqueeze(2).broadcast_to([P, R, K, E]),
                                        ALU.mult).then_inc(slot_k_done, 1)
                dve.wait_ge(slot_k_done, m + 1)
                with nc.allow_low_precision(reason="slot numbers are integers below 2^24"):
                    nc.vector.tensor_reduce(slot[:, par], slot_k[:].rearrange("p r k e -> p (r k) e"), X,
                                            ALU.add).then_inc(slot_done, 1)

            def route0(i, t, par):
                last = 1 - par
                if inside(i, 0):
                    dve.wait_ge(x_loaded[par], XL_ROUTE + 16 * (t + 1))
                    norm(0, i, par)
                if inside(i, 3):
                    place(0, i - 3, t - 2 + par, last)
                if inside(i, 2):
                    choose(0, i - 2, par)

            run_steps(dve, route0, STEPS + 3, first=4)

            def plan(f):
                at = PLAN * f

                def step(k, ins):
                    ins.then_inc(plan_dve, 1)
                    dve.wait_ge(plan_dve, at + k)

                dve.wait_ge(plan_pe, 3 * f + 1)
                step(1, nc.vector.tensor_copy(count_e[:], bank[2][0:E, 0:1]))
                step(2, nc.vector.tensor_scalar(reached[:], steps128[:], count_e[:], 0.0, ALU.is_lt, ALU.add,
                                                accum_out=blocks_e[:]))
                nc.vector.tensor_scalar(skip_e[:], blocks_e[:], -float(P), float(REGION), ALU.mult, ALU.add)
                dve.wait_ge(plan_pe, 3 * f + 2)
                step(3, nc.vector.tensor_copy(ends_e[:], bank[3][0:E, 0:1]))
                step(4, nc.vector.tensor_scalar(past[:], block_no[:], ends_e[:], None, ALU.is_ge))
                dve.wait_ge(plan_pe, 3 * f + 3)
                nc.vector.tensor_scalar(block_e[:], bank[2][0:1, 0:BLOCKS], float(E - 1), None, ALU.min)
                step(5, nc.vector.tensor_tensor(block_r[:], bank[3][0:1, 0:BLOCKS], block_row[:], ALU.add))
                nc.vector.memset(seen[:, 0], 0.0)

            def keep(f, k):
                every = flat(chosen[:])
                if k > 0:
                    dve.wait_ge(keep_dve, KEEP * f + k)

                def of(k):
                    return dict(out=weight[:, k].rearrange("p r i -> p i r"),
                                in1=kept[:, k].rearrange("p (r i) -> p i r", r=R),
                                scalar=0.5, op0=ALU.mult, op1=ALU.mult)

                if k == 0:
                    ins = nc.vector.tensor_tensor_scan(flat(incl[:]), flat(reset[:]), every, 0.0, ALU.mult, ALU.add)
                elif k == 1:
                    dve.wait_ge(keep_act, f + 1)
                    ins = nc.vector.tensor_reduce(rden[:].rearrange("p i r -> p (i r)"), exps[:], X, ALU.add)
                elif k == 2:
                    nc.vector.reciprocal(rden[:], rden[:])
                    dve.wait_ge(keep_pe, f + 1)
                    ins = nc.vector.tensor_copy(prefix[:], bank[6][:, 0:K * E])
                elif k == 3:
                    nc.vector.tensor_tensor(exp2[:], exp2[:], rden[:], ALU.mult)
                    ins = nc.vector.tensor_tensor(rank[:], incl[:],
                                                  prefix[:].unsqueeze(2).broadcast_to([P, K * E, R * STEPS]), ALU.add)
                elif k == 4:
                    ins = nc.vector.scalar_tensor_tensor(out=flat(rank[:]), in0=flat(rank[:]), scalar=float(CAPACITY),
                                                         in1=every, op0=ALU.is_le, op1=ALU.mult)
                elif k == 5:
                    ins = nc.vector.tensor_reduce(kept[:], rank[:].rearrange("p (k e) j -> p k j e", k=K), X, ALU.add)
                else:
                    nc.vector.scalar_tensor_tensor(in0=rden[:], **of(0))
                    ins = nc.vector.scalar_tensor_tensor(in0=exp2[:], **of(1))
                ins.then_inc(keep_dve, 1)

            def experts(f):
                N = BLOCKS * f

                def ids_of(g):
                    return slot_ids[:, bass.ds(G * g, G)]

                def to_gather(g, par, n):
                    dve.wait_ge(ids_loaded[par], 16 * G * (TURNS * f + n + 1))
                    nc.vector.tensor_scalar(gather_ids[:, par, :], ids_of(g), 1, None,
                                            ALU.logical_shift_right).then_inc(gather_ids_done, 1)

                def tick(b, t, u):
                    par, last = u % 2, (u + 1) % 2
                    if is_block(b, 1):
                        dve.wait_ge(hidT_in_psum, N + b)
                        wait(dve, y_in_psum, N + b - 2)
                        nc.vector.tensor_copy(flat(hidT[:, last]), bank[1][:, 0:D]).then_inc(hidT_ready, 1)
                    if is_block(b, 0):
                        dve.wait_ge(act_g_done, N + b + 1)
                        nc.vector.tensor_tensor(hid[:, par], act_g[:, par], bank[2 + par][:, D:],
                                                ALU.mult).then_inc(hid_done, 1)
                        if u % G == 0:
                            h, n = groups(t, u)
                            wait_apart(dve, (y_stored[h], 16 * G * (TURNS * f + n)))
                            nc.vector.tensor_copy(scatter_ids[:, h, :],
                                                  ids_of(2 * t + u // G)).then_inc(scatter_ids_done, 1)
                        if u % G == 2 and is_block(b, -2 * G + 2):
                            h, n = groups(t, u, 2)
                            dve.wait_ge(xgT_in_psum, N + b + 2)
                            to_gather(2 * t + u // G + 2, h, n)
                        if isinstance(b, int) and b < KEEP:
                            keep(f, b)

                for g in range(2):
                    to_gather(g, g, 0)
                run_blocks(dve, tick, 1)

            plan(0)
            phase_end(dve, 2)
            experts(0)
            phase_end(dve, 3)
            nc.vector.memset(e_sb[:, 1], 0.0).then_inc(e_zero, 1)

            def add_pairs(i, par, n):
                for r in range(R):
                    ins = nc.vector.scalar_tensor_tensor(
                        out=x_in[:, par, r, :], in0=pair_in[:, par, r, 0, :], scalar=weight[:, 0, r, bass.ds(i, 1)],
                        in1=x_in[:, par, r, :], op0=ALU.mult, op1=ALU.add)
                ins.then_inc(pair0_added, 1)
                dve.wait_ge(pair0_added, n + 1)
                for r in range(R):
                    ins = nc.vector.scalar_tensor_tensor(
                        out=x_in[:, par, r, :], in0=pair_in[:, par, r, 1, :], scalar=weight[:, 1, r, bass.ds(i, 1)],
                        in1=x_in[:, par, r, :], op0=ALU.mult, op1=ALU.add)
                return ins

            def ssm_input(i, t, par):
                if inside(i, 0):
                    dve.wait_ge(x_loaded[par], XL_SSM + 16 * (t + 1))
                    dve.wait_ge(pair_loaded[par], 16 * (t + 1))
                    add_pairs(i, par, i).then_inc(pair1_added, 1)
                    dve.wait_ge(pair1_added, i + 1)
                    layernorm(dve, LN_SSM + i, par)
                    normalize(dve, LN_SSM + i, par)
                if inside(i, 2):
                    dve.wait_ge(gelu_done, i - 1)
                    dve.wait_ge(sig_done, i - 1)
                    wait(dve, e_in_psum, i - 2)
                    nc.vector.tensor_tensor(flat(uT[:]), flat(gelu[:]), flat(sig[:]),
                                            ALU.mult).then_inc(uT_ready, 1)

            run_steps(dve, ssm_input, STEPS + 2, first=4)
            phase_end(dve, 4)

            for c in range(C):
                ins = nc.vector.tensor_copy(ends[:, c, :].rearrange("p (q r) -> p q r", r=R),
                                            e_sb[:, 1, c, :].rearrange("p (r q) -> p q r", r=R))
            ins.then_inc(ends_ready, 1)
            for k in range(LEVELS):
                width = CHUNKS - 2 ** k
                dve.wait_ge(ends_ready, k + 1)
                dve.wait_ge(level_in_psum, k + 1)
                for m in range(C):
                    later = ends[:, m, :].rearrange("p (b n) -> p b n", b=BATCHES)[:, :, 2 ** k:]
                    ins = nc.vector.tensor_tensor(
                        later, later, bank[6 + m][:, 0:BATCHES * width].rearrange("p (b n) -> p b n", b=BATCHES),
                        ALU.add)
                ins.then_inc(ends_ready, 1)
            dve.wait_ge(ends_ready, LEVELS + 1)
            per = P // BATCHES
            for c in range(C):
                nc.vector.tensor_copy(c_sb[:, 1, c, P:].rearrange("p (r q) -> p r q", r=R - 1),
                                      ends[:, c, :].rearrange("p (q r) -> p r q", r=R)[:, 0:R - 1, :])
                first = c_sb[:, 1, c, 0:P].rearrange("p (b q) -> p b q", b=BATCHES)
                nc.vector.tensor_copy(first[:, :, 1:],
                                      ends[:, c, :].rearrange("p (b q r) -> p b q r", b=BATCHES, r=R)[:, :, 0:per - 1, R - 1])
                ins = nc.vector.memset(first[:, :, 0:1], 0.0)
            ins.then_inc(carry_ready, 1)
            phase_end(dve, 5)

            def second_pass(i, t, par):
                last, tl = 1 - par, t - 1 + par
                if inside(i, 4):
                    place(1, i - 4, t - 2, par)
                if inside(i, 3):
                    choose(1, i - 3, last)
                if inside(i, 0):
                    dve.wait_ge(e_loaded[par], 16 * (t + 1))
                    dve.wait_ge(c_ready, i + 1)
                    nc.vector.tensor_tensor(flat(e_in[:, par]), flat(e_in[:, par]), flat(c_sb[:, par]),
                                            ALU.add).then_inc(s_ready, 1)
                if inside(i, 1):
                    dve.wait_ge(x_loaded[last], XL_SECOND + 16 * (tl + 1))
                    dve.wait_ge(ssm_in_psum, i)
                    for h in range(2):
                        x_h = flat(x_in[:, last, 2 * h:2 * h + 2])
                        ins = nc.vector.tensor_tensor(x_h, x_h, bank[6 + h][:], ALU.add)
                    ins.then_inc(x2_ready, 1)
                    dve.wait_ge(x2_ready, i)
                    norm(1, i - 1, last)

            run_steps(dve, second_pass, STEPS + 4, first=4)
            plan(1)
            phase_end(dve, 6)
            experts(1)
            phase_end(dve, 7)

            def last_pass(i, t, par):
                dve.wait_ge(x_loaded[par], XL_LAST + 16 * (t + 1))
                dve.wait_ge(pair_loaded[par], 8 * STEPS + 16 * (t + 1))
                add_pairs(i, par, STEPS + i).then_inc(out_ready, 1)

            run_steps(dve, last_pass)


_INS = ['L0_attn_x', 'L0_attn_W_u', 'L0_attn_b_u', 'L0_attn_W_g', 'L0_attn_b_g', 'L0_attn_A', 'L0_attn_Bm',
        'L0_attn_Cm', 'L0_attn_D', 'L0_ffn_router_w', 'L0_ffn_gate_w', 'L0_ffn_up_w', 'L0_ffn_down_w']
_OUTS = [((4, 2048, 256), 'float32')]


def kernel(**inputs):
    import numpy as _np
    import concourse.bacc as _bacc
    from concourse import mybir as _mybir
    from concourse.bass_utils import run_bass_kernel_spmd as _run

    nc = _bacc.Bacc("TRN2", target_bir_lowering=False, num_devices=1)
    arrays, args = {}, []
    for name in _INS:
        a = _np.ascontiguousarray(inputs[name])
        arrays[f"in_{name}_dram"] = a
        args.append(nc.dram_tensor(f"in_{name}_dram", a.shape, _mybir.dt.from_np(a.dtype), kind="ExternalInput").ap())
    for i, (shape, dtype) in enumerate(_OUTS):
        dt = _mybir.dt.from_np(_np.dtype(dtype))
        args.append(nc.dram_tensor(f"out_{i}_dram", shape, dt, kind="ExternalOutput").ap())
    macaron(nc, *args)
    r = _run(nc, [arrays], core_ids=[0])
    return r.results[0]["out_0_dram"]
```

```python
from contextlib import ExitStack

import concourse.bass as bass
from concourse import mybir

ALU = mybir.AluOpType
ACT = mybir.ActivationFunctionType
F32 = mybir.dt.float32
F32R = mybir.dt.float32r
BF16 = mybir.dt.bfloat16
U32 = mybir.dt.uint32
X = mybir.AxisListType.X

P = 128
R = 4
STEPS = 16
D = 256
C = D // P
E = 16
K = 2
TOKENS = 4 * 2048
COLS = R * P
BATCHES = 4
CHUNKS = TOKENS // STEPS // BATCHES
CAPACITY = -(-TOKENS * K * 5 // (E * 4))
REGION = TOKENS
BLOCKS = TOKENS * K // P + E
SLOTS = E * REGION + E * P
NOBODY = 1 << 20
UNDERFLOW = -104.0
EPS = 1e-5
PLAN, KEEP = 6, 7
SLOT_E = E // 2
W_COLS = 3 * D
U = 8
G = U // 2
TURNS = BLOCKS // U
SPAN = 2
LEAD = 3
LAG = 7
PAD = LAG - G
LEVELS = CHUNKS.bit_length() - 1
SQUARES = LEVELS + STEPS.bit_length() - 2


def wait(eng, sem, value):
    if not isinstance(value, int) or value > 0:
        eng.wait_ge(sem, value)


def run_steps(eng, tick, total=STEPS, first=2, split=None, done=0):
    for i in range(done, first):
        tick(i, i // 2, i % 2)
    bounds = [first // 2] + ([split // 2] if split else []) + [STEPS // 2]
    for lo, hi in zip(bounds, bounds[1:]):
        with eng.Fori(lo, hi) as t:
            for par in range(2):
                if split:
                    tick(2 * t + par, t, par, hi == split // 2)
                else:
                    tick(2 * t + par, t, par)
    for i in range(STEPS, total):
        tick(i, i // 2, i % 2)


def inside(i, lag):
    return not isinstance(i, int) or 0 <= i - lag < STEPS


def run_blocks(eng, tick, extra, first=1):
    for b in range(U * first):
        tick(b, b // U, b % U)
    with eng.Fori(first, TURNS - 1) as t:
        for u in range(U):
            tick(U * t + u, t, u)
    for u in range(U + extra):
        tick(BLOCKS - U + u, TURNS - 1 + u // U, u % U)


def groups(t, u, ahead=0):
    g = u // G + ahead
    return g % 2, t + g // 2


def is_block(b, lag):
    return not isinstance(b, int) or 0 <= b - lag < BLOCKS


def macaron(nc, x, W_u, b_u, W_g, b_g, A, Bm, Cm, Dv, router_w, gate_w, up_w, down_w, out):
    x_v = x.rearrange("b (q r i) d -> i (b q) r d", r=R, i=STEPS)
    out_v = out.rearrange("b (q r i) d -> i (b q) r d", r=R, i=STEPS)

    def dram(name, shape, dt):
        return nc.dram_tensor(name, shape, dt, kind="Internal").ap()

    xn_d = [dram(f"xn_d{f}", [TOKENS, D], F32) for f in range(2)]
    pair_d = [dram(f"pair_d{f}", [TOKENS * K, D], F32) for f in range(2)]
    slot_d = [dram(f"slot_d{f}", [SLOTS, 1], U32) for f in range(2)]
    x1_d = dram("x1_d", [STEPS, P, R * D], F32)
    x2_d = dram("x2_d", [STEPS, P, R * D], F32)
    e_d = dram("e_d", [STEPS, P, C * COLS], F32)
    split_d = dram("split_d", [SLOT_E, P, 2 * C * W_COLS], F32)
    pow_d = dram("pow_d", [SQUARES, P, C * D], F32)
    xn_v = [t.rearrange("(i p r) d -> i p (r d)", p=P, r=R) for t in xn_d]
    pair_v = [t.rearrange("(i p q) d -> i p (q d)", p=P, q=R * K) for t in pair_d]

    with ExitStack() as ctx:
        def sb(name, shape, dt):
            return ctx.enter_context(nc.sbuf_tensor(name, shape, dt))

        def sem(name):
            return ctx.enter_context(nc.semaphore(name))

        def sems(name, n):
            return [sem(f"{name}{i}") for i in range(n)]

        ring = sb("ring", [P, SLOT_E, 2, C, W_COLS], F32R)
        r_w = sb("r_w", [P, C, E], F32)
        wT = {n: sb(f"wT_{n}", [P, C, D], F32) for n in ("a", "c")}
        wT_split = {n: sb(f"wT_split_{n}", [P, 2, C, D], F32R) for n in ("u", "g", "b", "a")}
        bias_u = sb("bias_u", [P, C], F32)
        bias_g = sb("bias_g", [P, C], F32)
        d_row = sb("d_row", [P, D], F32)
        ident = sb("ident", [P, P], F32)
        before = sb("before", [P, P], BF16)
        ones = sb("ones", [P, P], BF16)
        reset = sb("reset", [P, K * E, R * STEPS], BF16)
        iota_e = sb("iota_e", [P, E], U32)
        region0 = sb("region0", [P, E], F32)
        pair_no = sb("pair_no", [P, STEPS, R * K], U32)
        steps128 = sb("steps128", [E, REGION // P], F32)
        upto = sb("upto", [E, E], F32)
        ones_e = sb("ones_e", [E, 1], F32)
        block_no = sb("block_no", [E, BLOCKS], F32)
        block_row = sb("block_row", [1, BLOCKS], F32)
        minus_half = sb("minus_half", [P, R], F32)
        key = sb("key", [P, STEPS, R, E], F32)
        key2 = sb("key2", [P, STEPS, R], F32)
        chosen = sb("chosen", [P, K, E, R, STEPS], BF16)
        weight = sb("weight", [P, K, R, STEPS], F32)
        slot_ids = sb("slot_ids", [P, BLOCKS], U32)
        gather_ids = sb("gather_ids", [P, 2, G], U32)
        scatter_ids = sb("scatter_ids", [P, 2, G], U32)
        block_e = sb("block_e", [1, LEAD + BLOCKS + 1], U32)
        block_r = sb("block_r", [1, BLOCKS], U32)
        done_upto = sb("done_upto", [1, PAD + BLOCKS], U32)
        xgT = sb("xgT", [P, 2, 2, C * P], F32R)
        hidT = sb("hidT", [P, 2, 2, C * P], F32R)
        stats = sb("stats", [P, R, 6], F32)
        mv = sb("mv", [P, R, 2], F32)
        var = sb("var", [P, R], F32)
        rstd = sb("rstd", [P, R], F32)
        std = sb("std", [P, R], F32)
        guess = sb("guess", [P, R], F32)
        square = sb("square", [P, R], F32)
        shift = sb("shift", [P, R], F32)
        top = sb("top", [P, R], F32)
        key_cur = sb("key_cur", [P, R, E], F32)
        max8 = sb("max8", [P, R, 8], F32)
        idx8 = sb("idx8", [P, R, 8], U32)
        either = sb("either", [P, R, E], BF16)
        seen = sb("seen", [P, 2, E], BF16)
        added = sb("added", [P, E], F32)
        slot_e = sb("slot_e", [P, R, E], F32)
        slot_k = sb("slot_k", [P, R, K, E], F32)
        slot = sb("slot", [P, 2, R * K], U32)
        pair_cur = sb("pair_cur", [P, 2, R * K], U32)
        count_e = sb("count_e", [E, 1], F32)
        reached = sb("reached", [E, REGION // P], F32)
        blocks_e = sb("blocks_e", [E, 1], F32)
        ends_e = sb("ends_e", [E, 1], F32)
        skip_e = sb("skip_e", [E, 1], F32)
        past = sb("past", [E, BLOCKS], F32)
        incl = sb("incl", [P, K * E, R * STEPS], BF16)
        prefix = sb("prefix", [P, K * E], F32)
        exp2 = sb("exp2", [P, STEPS, R], F32)
        rden = sb("rden", [P, STEPS, R], F32)
        kept = sb("kept", [P, K, R * STEPS], F32)

        work = sb("work", [P, 14 * 1024], F32)

        def part(at, shape):
            n = 1
            for s in shape:
                n *= s
            names = "abcd"[:len(shape)]
            pat = f"p ({' '.join(names)}) -> p {' '.join(names)}"
            return work[:, at:at + n].rearrange(pat, **dict(zip(names, shape)))

        x_in = part(0, [2, R, D])
        pair_in = part(2048, [2, R, K, D])
        xn = part(6144, [2, R, D])
        xnT = part(8192, [C, COLS])
        sig = part(9216, [C, COLS])
        gelu = part(10240, [2, C, COLS])
        e_sb = part(12288, [2, C, COLS])
        e_in = part(2048, [2, C, COLS])
        c_sb = part(4096, [2, C, COLS])
        ends = part(9216, [C, COLS])
        level_w = part(2048, [2, C, D])
        pw = part(5120, [C, D])
        pwT = part(5632, [C, D])

        def ring_part(at):
            return ring[:].rearrange("p s j c w -> p (s j c w)")[:, at:at + 2 * C * COLS].rearrange(
                "p (j c n) -> p j c n", j=2, c=C)

        xnT_split, uT_split, e_split = (ring_part(2 * C * COLS * k) for k in range(3))
        xg = part(8192, [U, D])
        y_sb = part(10240, [U, D])
        act_g = part(12288, [2, D])
        hid = part(12800, [2, D])
        rank = part(2048, [K * E, R * STEPS])
        exps = part(4096, [STEPS * R, E])
        raw_chunk = part(11264, [2, W_COLS])
        raw_w = part(2048, [2, C, W_COLS])
        split_w = part(11264, [2, C, W_COLS])
        raw = part(11264, [5, C, D])
        empty = part(9216, [1088]).bitcast(U32)

        bank = [ctx.enter_context(nc.psum_tensor(f"bank{i}", [P, 512], F32)) for i in range(8)]

        phase_done = sem("phase_done")
        const_step = sem("const_step")
        empty_ready = sem("empty_ready")
        refilled = sem("refilled")
        raw_loaded = sem("raw_loaded")
        small_loaded = sem("small_loaded")
        raw_w_loaded = sems("raw_w_loaded", 2)
        rounded_in_ring = sem("rounded_in_ring")
        split_saved = sem("split_saved")
        experts_split = sem("experts_split")
        router_loaded = sem("router_loaded")
        wT_in_psum = sem("wT_in_psum")
        wT_rounded = sem("wT_rounded")
        wT_ready = sem("wT_ready")
        x_loaded = sems("x_loaded", 2)
        pair_loaded = sems("pair_loaded", 2)
        e_loaded = sems("e_loaded", 2)
        stats_done = sem("stats_done")
        mv_done = sem("mv_done")
        var_done = sem("var_done")
        rstd_done = sem("rstd_done")
        std_done = sem("std_done")
        guess_done = sem("guess_done")
        square_done = sem("square_done")
        ratio_done = sem("ratio_done")
        shift_done = sem("shift_done")
        xn_ready = sem("xn_ready")
        xn_stored = sems("xn_stored", 2)
        xnT_in_psum = sem("xnT_in_psum")
        xnT_ready = sem("xnT_ready")
        logits_done = sem("logits_done")
        top_done = sem("top_done")
        key_done = sem("key_done")
        key_clamped = sem("key_clamped")
        max8_done = sem("max8_done")
        idx8_done = sem("idx8_done")
        chosen_done = sem("chosen_done")
        either_done = sem("either_done")
        added_done = sem("added_done")
        seen_done = sem("seen_done")
        slots_in_psum = sem("slots_in_psum")
        slot_e_done = sem("slot_e_done")
        slot_k_done = sem("slot_k_done")
        slot_done = sem("slot_done")
        slot_written = sems("slot_written", 2)
        square_in_psum = sem("square_in_psum")
        square_ready = sem("square_ready")
        square_stored = sem("square_stored")
        plan_pe = sem("plan_pe")
        plan_dve = sem("plan_dve")
        keep_pe = sem("keep_pe")
        keep_act = sem("keep_act")
        keep_dve = sem("keep_dve")
        ids_loaded = sems("ids_loaded", 2)
        gather_ids_done = sem("gather_ids_done")
        scatter_ids_done = sem("scatter_ids_done")
        xg_loaded = sems("xg_loaded", U)
        xgT_in_psum = sem("xgT_in_psum")
        xgT_rounded = sem("xgT_rounded")
        xgT_ready = sem("xgT_ready")
        gu_in_psum = sem("gu_in_psum")
        act_g_done = sem("act_g_done")
        hid_done = sem("hid_done")
        hidT_in_psum = sem("hidT_in_psum")
        hidT_rounded = sem("hidT_rounded")
        hidT_ready = sem("hidT_ready")
        y_in_psum = sem("y_in_psum")
        y_ready = sem("y_ready")
        y_stored = sems("y_stored", 2)
        pair0_added = sem("pair0_added")
        pair1_added = sem("pair1_added")
        x1_ready = sem("x1_ready")
        x1_stored = sems("x1_stored", 2)
        ug_in_psum = sem("ug_in_psum")
        sig_done = sem("sig_done")
        gelu_done = sem("gelu_done")
        xnT_rounded = sem("xnT_rounded")
        u_done = sem("u_done")
        uT_rounded = sem("uT_rounded")
        uT_ready = sem("uT_ready")
        e_zero = sem("e_zero")
        xg_zero = sem("xg_zero")
        e_in_psum = sem("e_in_psum")
        e_rounded = sem("e_rounded")
        e_ready = sem("e_ready")
        e_summed = sem("e_summed")
        e_stored = sems("e_stored", 2)
        ends_ready = sem("ends_ready")
        level_loaded = sems("level_loaded", 2)
        level_in_psum = sem("level_in_psum")
        carry_ready = sem("carry_ready")
        c_in_psum = sem("c_in_psum")
        c_ready = sem("c_ready")
        s_ready = sem("s_ready")
        ssm_in_psum = sem("ssm_in_psum")
        x2_ready = sem("x2_ready")
        x2_stored = sems("x2_stored", 2)
        out_ready = sem("out_ready")
        out_stored = sems("out_stored", 2)

        def phase_end(eng, k):
            eng.drain().then_inc(phase_done, 1)
            eng.wait_ge(phase_done, 5 * k)

        def wait_apart(eng, *waits):
            ready = [(sem, v if isinstance(v, int) else eng.compute_val(v)) for sem, v in waits
                     if not isinstance(v, int) or v > 0]
            eng.wait_ge(phase_done, 5)
            for sem, v in ready:
                eng.wait_ge(sem, v)

        LN_ROUTE, LN_SSM = (0, 2 * STEPS), STEPS
        XL_ROUTE, XL_SSM, XL_SECOND, XL_LAST = (16 * n * STEPS // 2 for n in range(4))

        def layernorm(dve, n, par):
            for r in range(R):
                ins = nc.vector.bn_stats(stats[:, r, :], x_in[:, par, r, :])
            ins.then_inc(stats_done, 1)
            wait_apart(dve, (stats_done, n + 1))
            for r in range(R):
                ins = nc.vector.bn_aggr(mv[:, r, :], stats[:, r, :])
            ins.then_inc(mv_done, 1)
            dve.wait_ge(mv_done, n + 1)
            wait(dve, rstd_done, n)
            nc.vector.tensor_scalar(var[:], mv[:, :, 1], EPS, None, ALU.add).then_inc(var_done, 1)

        def normalize(dve, n, par):
            wait(dve, xnT_in_psum, n - 1)
            dve.wait_ge(rstd_done, n + 1)
            for r in range(R):
                ins = nc.vector.tensor_scalar(xn[:, par, r, :], x_in[:, par, r, :], mv[:, r, 0:1],
                                              rstd[:, r:r + 1], ALU.subtract, ALU.mult)
            ins.then_inc(xn_ready, 1)

        def rstd_step(pool, n):
            pool.wait_ge(var_done, n + 1)
            wait(pool, xn_ready, n)
            nc.gpsimd.tensor_tensor(rstd[:], var[:], minus_half[:], ALU.pow).then_inc(rstd_done, 1)

        def turn_xn(pe, n, par):
            pe.wait_ge(xn_ready, n + 1)
            wait(pe, xnT_ready, n)
            for c in range(C):
                for r in range(R):
                    ins = nc.tensor.transpose(bank[c][:, r * P:(r + 1) * P],
                                              xn[:, par, r, c * P:(c + 1) * P], ident[:])
            ins.then_inc(xnT_in_psum, 1)

        def copy_xnT(act, n, users, used):
            act.wait_ge(xnT_in_psum, n + 1)
            wait(act, users, used)
            for c in range(C):
                ins = nc.scalar.copy(xnT[:, c, :], bank[c][:])
            ins.then_inc(xnT_ready, 1)

        def ends_of(h, c):
            half = BATCHES // 2
            return ends[:, c, :].rearrange("p (b n) -> p b n", b=BATCHES)[:, half * h:half * (h + 1), :]

        def level_part(h, m, width):
            half = BATCHES // 2
            return bank[4 + 2 * h + m][:, 0:half * width].rearrange("p (b n) -> p b n", b=half)

        def flat(ap):
            names = "abcd"[:len(ap.shape) - 1]
            return ap.rearrange(f"p {' '.join(names)} -> p ({' '.join(names)})")

        block = ctx.enter_context(nc.Block())

        @block.sync
        def _(sp):
            def load_x(i, t, par):
                wait(sp, xn_ready, i - 1)
                sp.dma_start(x_in[:, par], x_v[i]).then_inc(x_loaded[par], 16)

            load_x(0, 0, 0)
            for n, w in enumerate((W_u, W_g, Bm, A, Cm)):
                sp.dma_start(raw[:, n], w.rearrange("(c p) d -> p c d", p=P)).then_inc(raw_loaded, 16)
            sp.dma_start(pw[:], A.rearrange("(c p) d -> p c d", p=P)).then_inc(raw_loaded, 16)
            load_x(1, 0, 1)
            sp.dma_start(r_w[:], router_w.rearrange("(c p) e -> p c e", p=P)).then_inc(router_loaded, 16)
            for dst, b in ((bias_u, b_u), (bias_g, b_g)):
                for c in range(C):
                    sp.dma_start(dst[:, c:c + 1],
                                 b.rearrange("(c p a) -> c p a", p=P, a=1)[c]).then_inc(small_loaded, 16)
            sp.dma_start(d_row[:], Dv.rearrange("(a d) -> a d", a=1).broadcast_to([P, D])).then_inc(small_loaded, 16)
            phase_end(sp, 1)

            def store_xn(f, i, par):
                sp.dma_start(xn_v[f][i], flat(xn[:, par])).then_inc(xn_stored[par], 16)

            def store_power(k):
                sp.wait_ge(square_ready, k + 1)
                sp.dma_start(pow_d[k], flat(pwT[:])).then_inc(square_stored, 16)

            def load_route(i, t, par, squares=True):
                if inside(i, 0):
                    if inside(i, 2):
                        load_x(i, t, par)
                        sp.wait_ge(experts_split, 8 * (i - 1))
                    e = t if par else SLOT_E + t
                    for k, w in enumerate((gate_w, up_w, down_w)):
                        sp.dma_start(raw_w[:, par, :, k * D:(k + 1) * D],
                                     w[e].rearrange("(c p) h -> p c h", p=P)).then_inc(raw_w_loaded[par], 16)
                if inside(i, 2):
                    if not inside(i, 0):
                        sp.wait_ge(xn_ready, i - 1)
                    store_xn(0, i - 2, par)
                if inside(i, 2) and squares and not (isinstance(i, int) and i >= SQUARES):
                    store_power(i - 2)
                if inside(i, 2) and par == 0:
                    sp.wait_ge(experts_split, 8 * (i - 1))
                    wait(sp, split_saved, 16 * (t - 1))
                    sp.dma_start(split_d[t - 1], flat(split_w[:])).then_inc(split_saved, 16)

            run_steps(sp, load_route, STEPS + 2, first=4, split=SQUARES)
            store_power(SQUARES - 2)
            store_power(SQUARES - 1)
            sp.wait_ge(split_saved, 16 * SLOT_E)
            phase_end(sp, 2)

            def load_ids(f):
                def load(b, t, u):
                    par, n = groups(t, u)
                    if u % G == 0 and (f or not isinstance(b, int) or b >= U):
                        wait_apart(sp, (ids_loaded[par], 16 * G * (f * TURNS + n)))
                    row = sp.value_load(block_r[0:1, bass.ds(b, 1)], min_val=0, max_val=SLOTS - P)
                    sp.dma_start(slot_ids[:, bass.ds(b, 1)],
                                 slot_d[f][bass.ds(row, P), :]).then_inc(ids_loaded[par], 16)

                run_blocks(sp, load, 0)

            load_ids(0)
            for par in range(2):
                sp.dma_start(x_in[:, par], x_v[par]).then_inc(x_loaded[par], 16)
            phase_end(sp, 3)

            def load_ssm(i, t, par):
                if inside(i, 2):
                    wait(sp, x1_stored[par], 16 * t)
                    sp.dma_start(x_in[:, par], x_v[i]).then_inc(x_loaded[par], 16)
                wait(sp, pair1_added, i - 1)
                sp.dma_start(flat(pair_in[:, par]), pair_v[0][i]).then_inc(pair_loaded[par], 16)

            run_steps(sp, load_ssm)
            sp.wait_ge(pair1_added, STEPS)
            for k in range(LEVELS):
                wait(sp, level_in_psum, 2 * (k - 1))
                sp.dma_start(flat(level_w[:, k % 2]), pow_d[SQUARES - LEVELS + k]).then_inc(level_loaded[k % 2], 16)
            phase_end(sp, 4)

            def second_pass(i, t, par):
                if inside(i, 0):
                    if inside(i, 2):
                        sp.wait_ge(experts_split, 8 * (E + i - 1))
                    for k, w in enumerate((gate_w, up_w, down_w)):
                        sp.dma_start(raw_chunk[:, par, k * D:(k + 1) * D],
                                     w[t, par * P:(par + 1) * P, :]).then_inc(raw_w_loaded[par], 16)
                if inside(i, 2):
                    sp.wait_ge(x2_ready, 2 * (i - 1))
                    sp.dma_start(x2_d[i - 2], flat(x_in[:, par])).then_inc(x2_stored[par], 16)
                if inside(i, 0):
                    wait(sp, ssm_in_psum, 2 * (i - 1))
                    sp.dma_start(flat(e_in[:, par]), e_d[i]).then_inc(e_loaded[par], 16)
                    if inside(i, 2):
                        wait_apart(sp, (x2_stored[par], 16 * t),
                                   (xn_ready, LN_ROUTE[1] + i - 1))
                    sp.dma_start(flat(x_in[:, par]), x1_d[i]).then_inc(x_loaded[par], 16)
                if inside(i, 2):
                    if not inside(i, 0):
                        sp.wait_ge(xn_ready, LN_ROUTE[1] + i - 1)
                    store_xn(1, i - 2, par)

            run_steps(sp, second_pass, STEPS + 2)
            for par in range(2):
                sp.wait_ge(x2_stored[par], 8 * STEPS)
            phase_end(sp, 5)
            load_ids(1)
            for par in range(2):
                sp.dma_start(flat(x_in[:, par]), x2_d[par]).then_inc(x_loaded[par], 16)
            phase_end(sp, 6)

            def last_pass(i, t, par):
                if inside(i, 2):
                    sp.wait_ge(out_ready, i - 1)
                    sp.dma_start(out_v[i - 2], x_in[:, par]).then_inc(out_stored[par], 16)
                if inside(i, 0):
                    sp.dma_start(flat(pair_in[:, par]), pair_v[1][i]).then_inc(pair_loaded[par], 16)
                    if inside(i, 2):
                        sp.wait_ge(out_stored[par], 16 * t)
                        sp.dma_start(flat(x_in[:, par]), x2_d[i]).then_inc(x_loaded[par], 16)

            run_steps(sp, last_pass, STEPS + 2)
            for par in range(2):
                sp.wait_ge(out_stored[par], 8 * STEPS)

        @block.gpsimd
        def _(pool):
            nc.gpsimd.memset(empty[:], NOBODY).then_inc(empty_ready, 1)
            nc.gpsimd.memset(ident[:], 0.0)
            nc.gpsimd.memset(ones[:], 1.0)
            nc.gpsimd.memset(upto[:], 1.0)
            nc.gpsimd.memset(ones_e[:], 1.0)
            nc.gpsimd.memset(minus_half[:], -0.5)
            nc.gpsimd.memset(done_upto[:], 0)
            nc.gpsimd.memset(seen[:, 0], 0.0)
            nc.gpsimd.memset(before[:], 1.0)
            nc.gpsimd.memset(reset[:], 1.0).then_inc(const_step, 1)
            pool.wait_ge(const_step, 1)
            nc.gpsimd.affine_select(out=ident[:], in_=ident[:], compare_op=ALU.not_equal, fill=1.0,
                                    base=0, pattern=[[-1, P]], channel_multiplier=1)
            nc.gpsimd.affine_select(out=before[:], in_=before[:], compare_op=ALU.is_gt, fill=0.0,
                                    base=0, pattern=[[1, P]], channel_multiplier=-1)
            nc.gpsimd.affine_select(out=upto[:], in_=upto[:], compare_op=ALU.is_ge, fill=0.0,
                                    base=0, pattern=[[1, E]], channel_multiplier=-1)
            nc.gpsimd.memset(reset[:, :, 0:1], 0.0)
            nc.gpsimd.iota(iota_e[:], pattern=[[1, E]], base=0, channel_multiplier=0)
            nc.gpsimd.iota(region0[:], pattern=[[REGION, E]], base=0, channel_multiplier=0,
                           allow_small_or_imprecise_dtypes=True)
            nc.gpsimd.iota(pair_no[:], pattern=[[COLS * K, STEPS], [1, R * K]], base=0,
                           channel_multiplier=R * K)
            nc.gpsimd.iota(steps128[:], pattern=[[P, REGION // P]], base=0, channel_multiplier=0,
                           allow_small_or_imprecise_dtypes=True)
            nc.gpsimd.iota(block_no[:], pattern=[[1, BLOCKS]], base=0, channel_multiplier=0,
                           allow_small_or_imprecise_dtypes=True)
            nc.gpsimd.iota(block_row[:], pattern=[[P, BLOCKS]], base=0, channel_multiplier=0,
                           allow_small_or_imprecise_dtypes=True)
            phase_end(pool, 1)

            def write_slots(f, i, par):
                wait_apart(pool, (slot_done, STEPS * f + i + 1))
                for q in range(R * K):
                    nc.gpsimd.indirect_dma_start(
                        out=slot_d[f], out_offset=bass.IndirectOffsetOnAxis(ap=slot[:, par, q:q + 1], axis=0),
                        in_=pair_cur[:, par, q:q + 1], in_offset=None).then_inc(slot_written[par], 16)

            def all_written(f):
                for par in range(2):
                    pool.wait_ge(slot_written[par], 16 * R * K * (STEPS // 2) * (f + 1))

            pool.wait_ge(empty_ready, 1)
            for k in range(SLOT_E):
                slots = slot_d[k % 2].rearrange("(p q s) a -> q p (s a)", p=P, q=SLOT_E // 2)[k // 2]
                pool.dma_start(slots, empty[:, 0:2 * SLOTS // P // SLOT_E]).then_inc(refilled, 16)
            pool.wait_ge(refilled, 16 * SLOT_E)
            run_steps(pool, lambda i, t, par: write_slots(0, i, par))
            all_written(0)
            phase_end(pool, 2)

            def experts(f):
                pool.wait_ge(xg_zero, f + 1)

                def refill(b):
                    lo, hi = (pool.value_load(done_upto[0:1, bass.ds(b - d, 1)], min_val=0, max_val=SLOT_E)
                              for d in (2 * G, G))
                    with pool.If(lo < hi):
                        with pool.Fori(lo, hi) as j:
                            wait_apart(pool, (refilled, 16 * SLOT_E * (f + 1) + 16 * j))
                            pool.dma_start(flat(ring[:, j]), split_d[j]).then_inc(refilled, 16)

                def tick(b, t, u):
                    n = BLOCKS * f + b
                    if u % G == 0 and (not isinstance(b, int) or 8 <= b <= BLOCKS):
                        refill(b)
                    if is_block(b, 0):
                        if u % G == 0:
                            wait_apart(pool, (gather_ids_done, 2 * TURNS * f + 2 * t + u // G + 1))
                        wait_apart(pool, (xgT_in_psum, n - U + 1))
                        nc.gpsimd.indirect_dma_start(
                            out=xg[:, u], out_offset=None, in_=xn_d[f],
                            in_offset=bass.IndirectOffsetOnAxis(ap=gather_ids[:, u // G, u % G:u % G + 1], axis=0),
                            bounds_check=TOKENS - 1, oob_is_err=False).then_inc(xg_loaded[u], 16)
                    if is_block(b, LAG):
                        v, tv = (u - LAG) % U, t - (u < LAG)
                        if v % G == 0:
                            wait_apart(pool, (scatter_ids_done, 2 * TURNS * f + 2 * tv + v // G + 1))
                        wait_apart(pool, (y_ready, n - LAG + 1))
                        nc.gpsimd.indirect_dma_start(
                            out=pair_d[f],
                            out_offset=bass.IndirectOffsetOnAxis(ap=scatter_ids[:, v // G, v % G:v % G + 1], axis=0),
                            in_=y_sb[:, v], in_offset=None,
                            bounds_check=TOKENS * K - 1, oob_is_err=False).then_inc(y_stored[v // G], 16)

                run_blocks(pool, tick, LAG)
                for h in range(2):
                    pool.wait_ge(y_stored[h], 16 * G * TURNS * (f + 1))

            experts(0)
            phase_end(pool, 3)

            def ssm_input(i, t, par):
                last = 1 - par
                if inside(i, 2):
                    pool.wait_ge(gelu_done, i - 1)
                    pool.wait_ge(sig_done, i - 1)
                    nc.gpsimd.tensor_tensor(gelu[:, par], gelu[:, par], sig[:], ALU.mult).then_inc(u_done, 1)
                if inside(i, 0):
                    rstd_step(pool, LN_SSM + i)
                if inside(i, 3):
                    pool.wait_ge(e_ready, i - 2)
                    wait(pool, e_stored[last], 16 * (t - 2 + par))
                    nc.gpsimd.tensor_tensor(flat(e_sb[:, last]), flat(e_split[:, 0]).bitcast(F32),
                                            flat(e_split[:, 1]).bitcast(F32), ALU.add).then_inc(e_summed, 1)
                if inside(i, 0):
                    pool.wait_ge(xn_ready, LN_SSM + i + 1)
                    nc.gpsimd.tensor_tensor(x_in[:, par], x_in[:, par],
                                            d_row[:].unsqueeze(1).broadcast_to([P, R, D]),
                                            ALU.add).then_inc(x1_ready, 1)
                    wait_apart(pool, (x1_ready, i + 1))
                    pool.dma_start(x1_d[i], flat(x_in[:, par])).then_inc(x1_stored[par], 16)

            run_steps(pool, ssm_input, STEPS + 3, first=6)
            for par in range(2):
                pool.wait_ge(x1_stored[par], 8 * STEPS)
            phase_end(pool, 4)

            run_steps(pool, lambda i, t, par: write_slots(1, i, par))
            all_written(1)
            phase_end(pool, 5)
            experts(1)
            phase_end(pool, 6)

        @block.scalar
        def _(act):
            act.wait_ge(small_loaded, 80)
            phase_end(act, 1)
            act.wait_ge(wT_in_psum, 5)
            nc.scalar.copy(flat(wT["a"][:]), bank[3][:])
            nc.scalar.copy(flat(pwT[:]), bank[3][:])
            nc.scalar.copy(flat(wT["c"][:]), bank[4][:]).then_inc(wT_ready, 1)
            for n, name in enumerate("ugba"):
                nc.scalar.copy(flat(wT_split[name][:, 0]), bank[n][:]).then_inc(wT_rounded, 1)

            def exps_of_keys(f):
                act.wait_ge(seen_done, STEPS * (f + 1))
                nc.scalar.activation(exps[:], key[:].rearrange("p i r e -> p (i r) e"), ACT.Exp)
                nc.scalar.activation(exp2[:], key2[:], ACT.Exp).then_inc(keep_act, 1)

            def root(f, i):
                act.wait_ge(var_done, LN_ROUTE[f] + i + 1)
                nc.scalar.activation(std[:], var[:], ACT.Sqrt).then_inc(std_done, 1)

            def normalize_tiles(f, i, t, par):
                n = LN_ROUTE[f] + i
                act.wait_ge(shift_done, STEPS * f + i + 1)
                wait(act, xnT_in_psum, n - 1)
                if inside(i, 2):
                    act.wait_ge(xn_stored[par], 8 * STEPS * f + 16 * t)
                for r in range(R):
                    ins = nc.scalar.activation(xn[:, par, r, :], x_in[:, par, r, :], ACT.Identity,
                                               bias=shift[:, r:r + 1], scale=rstd[:, r:r + 1])
                ins.then_inc(xn_ready, 1)

            def copy_square(i):
                act.wait_ge(square_in_psum, i + 1)
                wait(act, square_stored, 16 * i)
                nc.scalar.copy(flat(pw[:]), bank[4][:])
                nc.scalar.copy(flat(pwT[:]), bank[5][:]).then_inc(square_ready, 1)

            def route0(i, t, par, squares=True):
                if inside(i, 0):
                    root(0, i)
                if inside(i, 1):
                    last, tl = 1 - par, t - 1 + par
                    act.wait_ge(raw_w_loaded[last], 16 * 3 * (tl + 1))
                    if par:
                        wait(act, split_saved, 16 * t)
                        rounded_w = flat(split_w[:, 0]).bitcast(F32R)
                    else:
                        rounded_w = flat(ring[:, t - 1, 0])
                    nc.scalar.copy(rounded_w, flat(raw_w[:, last])).then_inc(rounded_in_ring, 1)
                if inside(i, 0):
                    normalize_tiles(0, i, t, par)
                if inside(i, 1) and squares:
                    copy_square(i - 1)
                if inside(i, 0):
                    copy_xnT(act, LN_ROUTE[0] + i, logits_done, i)

            def route0_head(i, t, par, squares=True):
                route0(i, t, par, squares and not (isinstance(i, int) and i >= STEPS))

            run_steps(act, route0_head, STEPS + 1, first=4, split=SQUARES)
            copy_square(SQUARES - 1)
            act.wait_ge(square_stored, 16 * SQUARES)
            for par in range(2):
                act.wait_ge(xn_stored[par], 8 * STEPS)
            act.wait_ge(experts_split, 8 * E)
            exps_of_keys(0)
            phase_end(act, 2)

            def experts(f):
                N = BLOCKS * f

                def round_xgT(b, par):
                    act.wait_ge(xgT_in_psum, N + b + 1)
                    wait(act, gu_in_psum, N + b - 1)
                    nc.scalar.copy(xgT[:, par, 0], bank[7 * par][:, 0:D]).then_inc(xgT_rounded, 1)

                def tick(b, t, u):
                    par, last = u % 2, (u + 1) % 2
                    if is_block(b, 0):
                        act.wait_ge(gu_in_psum, N + b + 1)
                        wait(act, hid_done, N + b - 1)
                        nc.scalar.activation(act_g[:, par], bank[2 + par][:, 0:D],
                                             ACT.Silu).then_inc(act_g_done, 1)
                    if is_block(b, 1):
                        act.wait_ge(hidT_in_psum, N + b)
                        wait(act, y_in_psum, N + b - 2)
                        nc.scalar.copy(hidT[:, last, 0], bank[1 + 5 * last][:, 0:D]).then_inc(hidT_rounded, 1)
                    if is_block(b, -2):
                        round_xgT(b + 2, par)
                    if is_block(b, 2):
                        v, tv = (u - 2) % U, t - (u < 2)
                        if v % G == 0:
                            wait(act, y_stored[v // G], 16 * G * (TURNS * f + tv))
                        act.wait_ge(y_in_psum, N + b - 1)
                        nc.scalar.copy(y_sb[:, v], bank[4 + v % 2][:, 0:D]).then_inc(y_ready, 1)

                for b in range(2):
                    round_xgT(b, b)
                run_blocks(act, tick, 2)

            experts(0)
            phase_end(act, 3)

            def ssm_input(i, t, par):
                if inside(i, 1):
                    act.wait_ge(ug_in_psum, i)
                    wait(act, uT_ready, i - 2)
                    for m in range(C):
                        ins = nc.scalar.activation(gelu[:, 1 - par, m, :], bank[2 + m][:], ACT.Gelu,
                                                   bias=bias_u[:, m:m + 1])
                    ins.then_inc(gelu_done, 1)
                if inside(i, 0):
                    act.wait_ge(xnT_in_psum, LN_SSM + i + 1)
                    for c in range(C):
                        ins = nc.scalar.copy(xnT_split[:, 0, c, :], bank[c][:])
                    ins.then_inc(xnT_rounded, 1)
                if inside(i, 1):
                    wait(act, u_done, i - 1)
                    for m in range(C):
                        ins = nc.scalar.activation(sig[:, m, :], bank[4 + m][:], ACT.Sigmoid,
                                                   bias=bias_g[:, m:m + 1])
                    ins.then_inc(sig_done, 1)
                if inside(i, 2):
                    act.wait_ge(e_in_psum, i - 1)
                    wait(act, e_summed, i - 2)
                    for m in range(C):
                        ins = nc.scalar.copy(e_split[:, 0, m, :], bank[6 + m][:])
                    ins.then_inc(e_rounded, 1)
                if inside(i, 1):
                    act.wait_ge(u_done, i)
                    wait(act, e_in_psum, i - 1)
                    nc.scalar.copy(flat(uT_split[:, 0]), flat(gelu[:, 1 - par])).then_inc(uT_rounded, 1)
                if inside(i, 4):
                    act.wait_ge(e_summed, i - 3)
                    act.dma_start(e_d[i - 4], flat(e_sb[:, par])).then_inc(e_stored[par], 16)

            run_steps(act, ssm_input, STEPS + 4, first=4)
            for par in range(2):
                act.wait_ge(e_stored[par], 8 * STEPS)
            phase_end(act, 4)

            def second_pass(i, t, par):
                if inside(i, 2):
                    normalize_tiles(1, i - 2, t - 1, par)
                if inside(i, 0):
                    act.wait_ge(c_in_psum, i + 1)
                    wait(act, s_ready, i - 1)
                    for m in range(C):
                        ins = nc.scalar.copy(c_sb[:, par, m, :], bank[4 + m][:])
                    ins.then_inc(c_ready, 1)
                if inside(i, 2):
                    copy_xnT(act, LN_ROUTE[1] + i - 2, logits_done, STEPS + i - 2)
                if inside(i, 1):
                    root(1, i - 1)
                if inside(i, 0):
                    act.wait_ge(raw_w_loaded[par], 8 * STEPS * 3 + 16 * 3 * (t + 1))
                    nc.scalar.copy(ring[:, t, 0, par, :], raw_chunk[:, par]).then_inc(rounded_in_ring, 1)

            run_steps(act, second_pass, STEPS + 2, first=4)
            for par in range(2):
                act.wait_ge(xn_stored[par], 16 * STEPS)
            act.wait_ge(s_ready, STEPS)
            exps_of_keys(1)
            phase_end(act, 5)
            experts(1)
            phase_end(act, 6)

        @block.tensor
        def _(pe):
            pe.wait_ge(raw_loaded, 96)
            phase_end(pe, 1)
            for n in range(5):
                for k in range(C):
                    for m in range(C):
                        ins = nc.tensor.transpose(bank[n][:, k * D + m * P:k * D + (m + 1) * P],
                                                  raw[:, n, m, k * P:(k + 1) * P], ident[:])
                ins.then_inc(wT_in_psum, 1)
            pe.wait_ge(wT_ready, 5)
            pe.wait_ge(router_loaded, 16)

            def product(out_of, lhs, rhs, m_range=range(C)):
                for m in m_range:
                    for c in range(C):
                        ins = nc.tensor.matmul(out_of(m), lhs(c, m), rhs(c), start=(c == 0), stop=(c == C - 1))
                return ins

            def route_logits(f, i):
                pe.wait_ge(xnT_ready, LN_ROUTE[f] + i + 1)
                wait(pe, key_done, STEPS * f + i)
                for r in range(R):
                    for c in range(C):
                        ins = nc.tensor.matmul(bank[2][:, r * E:(r + 1) * E], xnT[:, c, r * P:(r + 1) * P],
                                               r_w[:, c, :], start=(c == 0), stop=(c == C - 1))
                ins.then_inc(logits_done, 1)

            def route_slots(f, i, par):
                n = STEPS * f + i
                pe.wait_ge(either_done, n + 1)
                wait(pe, seen_done, n)
                wait(pe, slot_e_done, n)
                place = bank[3][:, 0:R * E].rearrange("p (r e) -> p r e", r=R)
                nc.tensor.matmul(place, before[:], either[:], start=True, stop=False)
                for r in range(R - 1):
                    nc.tensor.matmul(place[:, r + 1:, :], ones[:],
                                     either[:, r:r + 1, :].broadcast_to([P, R - 1 - r, E]),
                                     start=False, stop=False)
                nc.tensor.matmul(place, ones[:], seen[:, par].unsqueeze(1).broadcast_to([P, R, E]),
                                 start=False, stop=True).then_inc(slots_in_psum, 1)

            def route0(i, t, par, squares=True):
                if inside(i, 0):
                    turn_xn(pe, LN_ROUTE[0] + i, par)
                    if squares:
                        wait(pe, square_ready, i)
                        product(lambda m: bank[4][:, m * D:(m + 1) * D],
                                lambda c, m: pwT[:, c, m * P:(m + 1) * P], lambda c: pw[:, c, :])
                        product(lambda m: bank[5][:, m * D:(m + 1) * D],
                                lambda c, m: pw[:, c, m * P:(m + 1) * P],
                                lambda c: pwT[:, c, :]).then_inc(square_in_psum, 1)
                    route_logits(0, i)
                if inside(i, 1):
                    route_slots(0, i - 1, 1 - par)

            run_steps(pe, route0, STEPS + 1, split=SQUARES)

            def plan(f):
                at = PLAN * f
                pe.wait_ge(seen_done, STEPS * (f + 1))
                if f == 0:
                    pe.wait_ge(square_ready, SQUARES)
                else:
                    pe.wait_ge(c_ready, STEPS)
                pe.wait_ge(xnT_ready, LN_ROUTE[f] + STEPS)
                nc.tensor.matmul(bank[4][0:E, 0:1], seen[:, 0], ones[:, 0:1], start=True,
                                 stop=True).then_inc(plan_pe, 1)
                pe.wait_ge(plan_dve, at + 3)
                nc.tensor.matmul(bank[5][0:E, 0:1], upto[:], blocks_e[:], start=True,
                                 stop=True).then_inc(plan_pe, 1)
                pe.wait_ge(plan_dve, at + 5)
                nc.tensor.matmul(bank[4][0:1, 0:BLOCKS], ones_e[:], past[:], start=True, stop=True)
                nc.tensor.matmul(bank[5][0:1, D:D + BLOCKS], upto[:, SLOT_E - 1:SLOT_E], past[:], start=True, stop=True)
                nc.tensor.matmul(bank[5][0:1, 0:BLOCKS], skip_e[:], past[:], start=True,
                                 stop=True).then_inc(plan_pe, 1)
                pe.wait_ge(keep_dve, KEEP * f + 1)
                nc.tensor.matmul(bank[0][:, 0:K * E], before[:], incl[:, :, R * STEPS - 1], start=True,
                                 stop=True).then_inc(keep_pe, 1)

            def experts(f):
                N = BLOCKS * f
                pe.wait_ge(experts_split, 8 * E * (f + 1))

                def turn_xg(b, t, u):
                    pe.wait_ge(xg_loaded[u], 16 * (TURNS * f + t + 1))
                    wait(pe, xgT_ready, N + b - 1)
                    for c in range(C):
                        ins = nc.tensor.transpose(bank[7 * (u % 2)][:, c * P:(c + 1) * P],
                                                  xg[:, u, c * P:(c + 1) * P], ident[:])
                    ins.then_inc(xgT_in_psum, 1)

                def split_product(out, xT, w):
                    terms = [(c, i, j) for c in range(C) for i, j in ((0, 0), (1, 0), (0, 1))]
                    for n, (c, i, j) in enumerate(terms):
                        ins = nc.tensor.matmul(out, xT[:, i, c * P:(c + 1) * P], w(j, c),
                                               start=(n == 0), stop=(n == len(terms) - 1))
                    return ins

                expert = {}

                def load_experts(b, v, n):
                    _, e = nc.values_load_multi_w_load_instructions(
                        block_e[0:1, bass.ds(LEAD + b, n)], engines=(mybir.EngineType.PE,), min_val=0, max_val=E - 1)
                    for k in range(n):
                        expert[(v + k) % (SPAN * U)] = e[k]

                def tick(b, t, u, v):
                    par, last = u % 2, (u + 1) % 2
                    if is_block(b, 0):
                        if v == 0 and is_block(b, LEAD):
                            load_experts(b - LEAD, v - LEAD, 8)
                        elif v == 0:
                            load_experts(b, v, 5)
                        elif v % 4 == 1 and v > 1:
                            load_experts(b, v, 3 if isinstance(b, int) and b + 3 > BLOCKS - 1 else 4)
                        e = expert[v]
                        pe.wait_ge(refilled, 16 * (SLOT_E * f + 1) + 16 * e)
                    if is_block(b, 2):
                        pe.wait_ge(hid_done, N + b - 1)
                        wait(pe, hidT_ready, N + b - 3)
                        for c in range(C):
                            ins = nc.tensor.transpose(bank[1 + 5 * par][:, c * P:(c + 1) * P],
                                                      hid[:, par, c * P:(c + 1) * P], ident[:])
                        ins.then_inc(hidT_in_psum, 1)
                    if is_block(b, -1):
                        turn_xg(b + 1, t + (u + 1) // U, (u + 1) % U)
                    if is_block(b, 3):
                        pe.wait_ge(hidT_ready, N + b - 2)
                        wait(pe, y_ready, N + b - 4)
                        j = expert[(v - 3) % (SPAN * U)] % SLOT_E
                        split_product(bank[4 + last][:, 0:D], hidT[:, last],
                                      lambda i, c: ring[:, j, i, c, 2 * D:]).then_inc(y_in_psum, 1)
                    if is_block(b, 0):
                        pe.wait_ge(xgT_ready, N + b + 1)
                        wait(pe, hid_done, N + b - 1)
                        k = expert[v] % SLOT_E
                        split_product(bank[2 + par][:], xgT[:, par],
                                      lambda i, c: ring[:, k, i, c, 0:2 * D]).then_inc(gu_in_psum, 1)

                turn_xg(0, 0, 0)
                for b in range(U):
                    tick(b, 0, b, b)
                with pe.Fori(0, (TURNS - 2) // SPAN) as w:
                    for v in range(SPAN * U):
                        tick(U + SPAN * U * w + v, 1 + SPAN * w + v // U, v % U, v)
                for u in range(U + LEAD):
                    tick(BLOCKS - U + u, TURNS - 1 + u // U, u % U, u)

            plan(0)
            phase_end(pe, 2)
            experts(0)
            phase_end(pe, 3)
            pe.wait_ge(e_zero, 3)

            def split_terms(m, name, xT):
                return [(wT_split[name][:, j, c, m * P:(m + 1) * P], xT[:, i, c, :])
                        for c in range(C) for i, j in ((0, 0), (1, 0), (0, 1))]

            def sum_of(out, terms):
                for n, (lhs, rhs) in enumerate(terms):
                    ins = nc.tensor.matmul(out, lhs, rhs, start=(n == 0), stop=(n == len(terms) - 1))
                return ins

            def weight_of(name):
                return lambda c, m: wT[name][:, c, m * P:(m + 1) * P]

            def ssm_input(i, t, par):
                if inside(i, 1):
                    pe.wait_ge(xnT_ready, LN_SSM + i)
                    wait(pe, gelu_done, i - 1)
                    wait(pe, sig_done, i - 1)
                    for m in range(C):
                        sum_of(bank[2 + m][:], split_terms(m, "u", xnT_split))
                        ins = sum_of(bank[4 + m][:], split_terms(m, "g", xnT_split))
                    ins.then_inc(ug_in_psum, 1)
                if inside(i, 0):
                    turn_xn(pe, LN_SSM + i, par)
                if inside(i, 2):
                    pe.wait_ge(uT_ready, i - 1)
                    wait(pe, e_ready, i - 2)
                    for m in range(C):
                        ins = sum_of(bank[6 + m][:], split_terms(m, "b", uT_split) + split_terms(m, "a", e_split))
                    ins.then_inc(e_in_psum, 1)

            run_steps(pe, ssm_input, STEPS + 2, first=4)
            for k in range(LEVELS):
                width = CHUNKS - 2 ** k
                pe.wait_ge(level_loaded[k % 2], 16 * (k // 2 + 1))
                for h in range(2):
                    pe.wait_ge(ends_ready, 2 * k + h + 1)
                    for m in range(C):
                        for c in range(C):
                            ins = nc.tensor.matmul(
                                level_part(h, m, width), level_w[:, k % 2, c, m * P:(m + 1) * P],
                                ends_of(h, c)[:, :, 0:width], start=(c == 0), stop=(c == C - 1))
                    ins.then_inc(level_in_psum, 1)
            phase_end(pe, 4)
            pe.wait_ge(carry_ready, 1)

            def second_pass(i, t, par):
                last = 1 - par
                if inside(i, 0):
                    wait(pe, c_ready, i)
                    product(lambda m: bank[4 + m][:], weight_of("a"),
                            lambda c: c_sb[:, last, c, :]).then_inc(c_in_psum, 1)
                if inside(i, 2):
                    turn_xn(pe, LN_ROUTE[1] + i - 2, par)
                if inside(i, 1):
                    pe.wait_ge(s_ready, i)
                    wait(pe, x2_ready, 2 * (i - 1))
                    for r in range(R):
                        for c in range(C):
                            ins = nc.tensor.matmul(bank[6 + r // 2][:, (r % 2) * D:(r % 2 + 1) * D],
                                                   e_in[:, last, c, r * P:(r + 1) * P], wT["c"][:, c, :],
                                                   start=(c == 0), stop=(c == C - 1))
                        if r % 2 == 1:
                            ins.then_inc(ssm_in_psum, 1)
                if inside(i, 2):
                    route_logits(1, i - 2)
                if inside(i, 3):
                    route_slots(1, i - 3, last)

            run_steps(pe, second_pass, STEPS + 3, first=4)
            plan(1)
            phase_end(pe, 5)
            experts(1)
            phase_end(pe, 6)

        @block.vector
        def _(dve):
            phase_end(dve, 1)

            def rest_of(out, whole, rounded, done):
                nc.vector.tensor_tensor(out, whole, rounded.bitcast(F32), ALU.subtract).then_inc(done, 1)

            for n, name in enumerate("ugba"):
                dve.wait_ge(wT_rounded, n + 1)
                rest_of(flat(wT_split[name][:, 1]), bank[n][:], flat(wT_split[name][:, 0]), wT_ready)

            def norm_stats(par, tiles):
                for r in tiles:
                    ins = nc.vector.bn_stats(stats[:, r, :], x_in[:, par, r, :])
                return ins

            def norm(f, i, par, tiles=range(R)):
                n = LN_ROUTE[f] + i
                norm_stats(par, tiles).then_inc(stats_done, 1)
                wait_apart(dve, (stats_done, n + 1))
                for r in range(R):
                    ins = nc.vector.bn_aggr(mv[:, r, :], stats[:, r, :])
                ins.then_inc(mv_done, 1)
                dve.wait_ge(mv_done, n + 1)
                nc.vector.tensor_scalar(var[:], mv[:, :, 1], EPS, None, ALU.add).then_inc(var_done, 1)

            def norm_end(f, i):
                n, k = LN_ROUTE[f] + i, STEPS * f + i
                dve.wait_ge(std_done, k + 1)
                nc.vector.reciprocal(guess[:], std[:]).then_inc(guess_done, 1)
                dve.wait_ge(guess_done, k + 1)
                nc.vector.tensor_tensor(square[:], guess[:], guess[:], ALU.mult).then_inc(square_done, 1)
                dve.wait_ge(square_done, k + 1)
                nc.vector.scalar_tensor_tensor(out=square[:], in0=square[:], scalar=-0.5, in1=var[:],
                                               op0=ALU.mult, op1=ALU.mult).then_inc(ratio_done, 1)
                wait(dve, xn_ready, n)
                dve.wait_ge(ratio_done, k + 1)
                nc.vector.scalar_tensor_tensor(out=rstd[:], in0=square[:], scalar=1.5, in1=guess[:],
                                               op0=ALU.add, op1=ALU.mult).then_inc(rstd_done, 1)
                dve.wait_ge(rstd_done, n + 1)
                nc.vector.scalar_tensor_tensor(out=shift[:], in0=mv[:, :, 0], scalar=-1.0, in1=rstd[:],
                                               op0=ALU.mult, op1=ALU.mult).then_inc(shift_done, 1)

            def choose(f, i, par):
                m = STEPS * f + i
                lg = bank[2][:, 0:R * E].rearrange("p (r e) -> p r e", r=R)
                dve.wait_ge(logits_done, m + 1)
                nc.vector.tensor_reduce(top[:], lg, X, ALU.max).then_inc(top_done, 1)
                dve.wait_ge(top_done, m + 1)
                nc.vector.tensor_tensor(key_cur[:], lg, top[:].unsqueeze(2).broadcast_to([P, R, E]),
                                        ALU.subtract).then_inc(key_done, 1)
                dve.wait_ge(key_done, m + 1)
                nc.vector.tensor_scalar(key_cur[:], key_cur[:], UNDERFLOW, None, ALU.max).then_inc(key_clamped, 1)
                wait_apart(dve, (key_clamped, m + 1))
                for r in range(R):
                    ins = nc.vector.max(max8[:, r, :], key_cur[:, r, :])
                ins.then_inc(max8_done, 1)
                nc.vector.tensor_copy(key[:, i], key_cur[:])
                wait_apart(dve, (max8_done, m + 1))
                for r in range(R):
                    ins = nc.vector.max_index(idx8[:, r, :], max8[:, r, :], key_cur[:, r, :])
                ins.then_inc(idx8_done, 1)
                nc.vector.tensor_copy(key2[:, i], max8[:, :, 1])
                dve.wait_ge(idx8_done, m + 1)
                nc.vector.tensor_tensor(
                    chosen[:, :, :, :, i].rearrange("p k e r -> p k r e"),
                    idx8[:, :, 0:K].rearrange("p r k -> p k r").unsqueeze(3).broadcast_to([P, K, R, E]),
                    iota_e[:].unsqueeze(1).unsqueeze(1).broadcast_to([P, K, R, E]), ALU.is_equal).then_inc(chosen_done, 1)
                dve.wait_ge(chosen_done, m + 1)
                wait(dve, slots_in_psum, m)
                nc.vector.tensor_tensor(either[:], chosen[:, 0, :, :, i].rearrange("p e r -> p r e"),
                                        chosen[:, 1, :, :, i].rearrange("p e r -> p r e"),
                                        ALU.add).then_inc(either_done, 1)
                dve.wait_ge(either_done, m + 1)
                nc.vector.tensor_reduce(added[:], either[:].rearrange("p r e -> p e r"), X,
                                        ALU.add).then_inc(added_done, 1)
                dve.wait_ge(added_done, m + 1)
                nc.vector.tensor_tensor(seen[:, 1 - par], seen[:, par], added[:], ALU.add).then_inc(seen_done, 1)

            def place(f, i, t, par):
                m = STEPS * f + i
                wait_apart(dve, (slot_written[par], 16 * R * K * (STEPS // 2 * f + t)))
                nc.vector.tensor_copy(pair_cur[:, par], pair_no[:, i])
                dve.wait_ge(slots_in_psum, m + 1)
                nc.vector.tensor_tensor(slot_e[:], bank[3][:, 0:R * E].rearrange("p (r e) -> p r e", r=R),
                                        region0[:].unsqueeze(1).broadcast_to([P, R, E]),
                                        ALU.add).then_inc(slot_e_done, 1)
                dve.wait_ge(slot_e_done, m + 1)
                nc.vector.tensor_tensor(slot_k[:], chosen[:, :, :, :, i].rearrange("p k e r -> p r k e"),
                                        slot_e[:].unsqueeze(2).broadcast_to([P, R, K, E]),
                                        ALU.mult).then_inc(slot_k_done, 1)
                dve.wait_ge(slot_k_done, m + 1)
                with nc.allow_low_precision(reason="slot numbers are integers below 2^24"):
                    nc.vector.tensor_reduce(slot[:, par], slot_k[:].rearrange("p r k e -> p (r k) e"), X,
                                            ALU.add).then_inc(slot_done, 1)

            def route0(i, t, par):
                last = 1 - par
                if inside(i, 0):
                    dve.wait_ge(x_loaded[par], XL_ROUTE + 16 * (t + 1))
                    norm(0, i, par)
                if inside(i, 2):
                    choose(0, i - 2, par)
                if inside(i, 0):
                    norm_end(0, i)
                if inside(i, 1):
                    dve.wait_ge(rounded_in_ring, i)
                    w0, w1 = ((split_w[:, k] if par else ring[:, t - 1, k]) for k in range(2))
                    nc.vector.tensor_tensor(flat(w1).bitcast(F32R), flat(raw_w[:, last]), flat(w0).bitcast(F32),
                                            ALU.subtract).then_inc(experts_split, 8)
                if inside(i, 3):
                    place(0, i - 3, t - 2 + par, last)

            run_steps(dve, route0, STEPS + 2, first=4)

            def plan(f):
                at = PLAN * f

                def step(k, ins):
                    ins.then_inc(plan_dve, 1)
                    dve.wait_ge(plan_dve, at + k)

                dve.wait_ge(plan_pe, 3 * f + 1)
                step(1, nc.vector.tensor_copy(count_e[:], bank[4][0:E, 0:1]))
                step(2, nc.vector.tensor_scalar(reached[:], steps128[:], count_e[:], 0.0, ALU.is_lt, ALU.add,
                                                accum_out=blocks_e[:]))
                step(3, nc.vector.tensor_scalar(blocks_e[:], blocks_e[:], 1.0, None, ALU.max))
                nc.vector.tensor_scalar(skip_e[:], blocks_e[:], -float(P), float(REGION), ALU.mult, ALU.add)
                dve.wait_ge(plan_pe, 3 * f + 2)
                step(4, nc.vector.tensor_copy(ends_e[:], bank[5][0:E, 0:1]))
                step(5, nc.vector.tensor_scalar(past[:], block_no[:], ends_e[:], None, ALU.is_ge))
                dve.wait_ge(plan_pe, 3 * f + 3)
                nc.vector.tensor_scalar(block_e[:, LEAD:LEAD + BLOCKS], bank[4][0:1, 0:BLOCKS], float(E - 1), None, ALU.min)
                nc.vector.tensor_copy(done_upto[:, PAD:], bank[5][0:1, D:D + BLOCKS])
                step(6, nc.vector.tensor_tensor(block_r[:], bank[5][0:1, 0:BLOCKS], block_row[:], ALU.add))
                nc.vector.memset(seen[:, 0], 0.0)

            def keep(f, k):
                every = flat(chosen[:])
                if k > 0:
                    dve.wait_ge(keep_dve, KEEP * f + k)

                def of(k):
                    return dict(out=weight[:, k].rearrange("p r i -> p i r"),
                                in1=kept[:, k].rearrange("p (r i) -> p i r", r=R),
                                scalar=0.5, op0=ALU.mult, op1=ALU.mult)

                if k == 0:
                    ins = nc.vector.tensor_tensor_scan(flat(incl[:]), flat(reset[:]), every, 0.0, ALU.mult, ALU.add)
                elif k == 1:
                    dve.wait_ge(keep_act, f + 1)
                    ins = nc.vector.tensor_reduce(rden[:].rearrange("p i r -> p (i r)"), exps[:], X, ALU.add)
                elif k == 2:
                    nc.vector.reciprocal(rden[:], rden[:])
                    dve.wait_ge(keep_pe, f + 1)
                    ins = nc.vector.tensor_copy(prefix[:], bank[0][:, 0:K * E])
                elif k == 3:
                    nc.vector.tensor_tensor(exp2[:], exp2[:], rden[:], ALU.mult)
                    ins = nc.vector.tensor_tensor(rank[:], incl[:],
                                                  prefix[:].unsqueeze(2).broadcast_to([P, K * E, R * STEPS]), ALU.add)
                elif k == 4:
                    ins = nc.vector.scalar_tensor_tensor(out=flat(rank[:]), in0=flat(rank[:]), scalar=float(CAPACITY),
                                                         in1=every, op0=ALU.is_le, op1=ALU.mult)
                elif k == 5:
                    ins = nc.vector.tensor_reduce(kept[:], rank[:].rearrange("p (k e) j -> p k j e", k=K), X, ALU.add)
                else:
                    nc.vector.scalar_tensor_tensor(in0=rden[:], **of(0))
                    ins = nc.vector.scalar_tensor_tensor(in0=exp2[:], **of(1))
                ins.then_inc(keep_dve, 1)

            def routed(f):
                plan(f)
                for k in range(KEEP - 3):
                    keep(f, k)
                place(f, STEPS - 1, STEPS // 2 - 1, 1)
                for k in range(KEEP - 3, KEEP):
                    keep(f, k)
                nc.vector.memset(xg[:], 0.0).then_inc(xg_zero, 1)

            def experts(f):
                N = BLOCKS * f

                def ids_of(g):
                    return slot_ids[:, bass.ds(G * g, G)]

                def to_gather(g, par, n):
                    dve.wait_ge(ids_loaded[par], 16 * G * (TURNS * f + n + 1))
                    nc.vector.tensor_scalar(gather_ids[:, par, :], ids_of(g), 1, None,
                                            ALU.logical_shift_right).then_inc(gather_ids_done, 1)

                def rest_of_xgT(b, par):
                    dve.wait_ge(xgT_rounded, N + b + 1)
                    nc.vector.tensor_tensor(xgT[:, par, 1], bank[7 * par][:, 0:D], xgT[:, par, 0].bitcast(F32),
                                            ALU.subtract).then_inc(xgT_ready, 1)

                def tick(b, t, u):
                    par, last = u % 2, (u + 1) % 2
                    if is_block(b, 0):
                        dve.wait_ge(act_g_done, N + b + 1)
                        nc.vector.tensor_tensor(hid[:, par], act_g[:, par], bank[2 + par][:, D:],
                                                ALU.mult).then_inc(hid_done, 1)
                    if is_block(b, 1):
                        dve.wait_ge(hidT_rounded, N + b)
                        nc.vector.tensor_tensor(hidT[:, last, 1], bank[1 + 5 * last][:, 0:D],
                                                hidT[:, last, 0].bitcast(F32), ALU.subtract).then_inc(hidT_ready, 1)
                    if is_block(b, -2):
                        rest_of_xgT(b + 2, par)
                    if is_block(b, 0):
                        if u % G == 0:
                            h, n = groups(t, u)
                            wait_apart(dve, (y_stored[h], 16 * G * (TURNS * f + n)))
                            nc.vector.tensor_copy(scatter_ids[:, h, :],
                                                  ids_of(2 * t + u // G)).then_inc(scatter_ids_done, 1)
                        if u % G == 2 and is_block(b, -2 * G + 2):
                            h, n = groups(t, u, 2)
                            dve.wait_ge(xgT_in_psum, N + b + 2)
                            to_gather(2 * t + u // G + 2, h, n)

                for g in range(2):
                    to_gather(g, g, 0)
                for b in range(2):
                    rest_of_xgT(b, b)
                run_blocks(dve, tick, 1)

            routed(0)
            phase_end(dve, 2)
            experts(0)
            phase_end(dve, 3)
            nc.vector.memset(e_sb[:, 1], 0.0).then_inc(e_zero, 1)
            dve.wait_ge(e_zero, 1)
            for j in range(2):
                nc.vector.tensor_copy(flat(e_split[:, j]), flat(e_sb[:, 1])).then_inc(e_zero, 1)

            def add_pairs(i, par, n):
                for r in range(R):
                    ins = nc.vector.scalar_tensor_tensor(
                        out=x_in[:, par, r, :], in0=pair_in[:, par, r, 0, :], scalar=weight[:, 0, r, bass.ds(i, 1)],
                        in1=x_in[:, par, r, :], op0=ALU.mult, op1=ALU.add)
                ins.then_inc(pair0_added, 1)
                dve.wait_ge(pair0_added, n + 1)
                for r in range(R):
                    ins = nc.vector.scalar_tensor_tensor(
                        out=x_in[:, par, r, :], in0=pair_in[:, par, r, 1, :], scalar=weight[:, 1, r, bass.ds(i, 1)],
                        in1=x_in[:, par, r, :], op0=ALU.mult, op1=ALU.add)
                return ins

            def ssm_input(i, t, par):
                if inside(i, 1):
                    dve.wait_ge(xnT_rounded, i)
                    for c in range(C):
                        ins = nc.vector.tensor_tensor(xnT_split[:, 1, c, :], bank[c][:],
                                                      xnT_split[:, 0, c, :].bitcast(F32), ALU.subtract)
                    ins.then_inc(xnT_ready, 1)
                if inside(i, 0):
                    dve.wait_ge(x_loaded[par], XL_SSM + 16 * (t + 1))
                    dve.wait_ge(pair_loaded[par], 16 * (t + 1))
                    add_pairs(i, par, i).then_inc(pair1_added, 1)
                    dve.wait_ge(pair1_added, i + 1)
                    layernorm(dve, LN_SSM + i, par)
                if inside(i, 3):
                    dve.wait_ge(e_rounded, i - 2)
                    for m in range(C):
                        ins = nc.vector.tensor_tensor(e_split[:, 1, m, :], bank[6 + m][:],
                                                      e_split[:, 0, m, :].bitcast(F32), ALU.subtract)
                    ins.then_inc(e_ready, 1)
                if inside(i, 0):
                    normalize(dve, LN_SSM + i, par)
                if inside(i, 2):
                    dve.wait_ge(uT_rounded, i - 1)
                    rest_of(flat(uT_split[:, 1]), flat(gelu[:, par]), flat(uT_split[:, 0]), uT_ready)

            run_steps(dve, ssm_input, STEPS + 3, first=4)

            dve.wait_ge(e_ready, STEPS)
            dve.wait_ge(u_done, STEPS)
            for c in range(C):
                ins = nc.vector.tensor_tensor(ends[:, c, :].rearrange("p (q r) -> p q r", r=R),
                                              e_split[:, 0, c, :].bitcast(F32).rearrange("p (r q) -> p q r", r=R),
                                              e_split[:, 1, c, :].bitcast(F32).rearrange("p (r q) -> p q r", r=R), ALU.add)
            ins.then_inc(ends_ready, 2)
            for k in range(LEVELS):
                for h in range(2):
                    dve.wait_ge(level_in_psum, 2 * k + h + 1)
                    for m in range(C):
                        later = ends_of(h, m)[:, :, 2 ** k:]
                        ins = nc.vector.tensor_tensor(later, later, level_part(h, m, CHUNKS - 2 ** k), ALU.add)
                    ins.then_inc(ends_ready, 1)
            dve.wait_ge(ends_ready, 2 * LEVELS + 2)
            per = P // BATCHES
            for c in range(C):
                nc.vector.tensor_copy(c_sb[:, 1, c, P:].rearrange("p (r q) -> p r q", r=R - 1),
                                      ends[:, c, :].rearrange("p (q r) -> p r q", r=R)[:, 0:R - 1, :])
                first = c_sb[:, 1, c, 0:P].rearrange("p (b q) -> p b q", b=BATCHES)
                nc.vector.tensor_copy(first[:, :, 1:],
                                      ends[:, c, :].rearrange("p (b q r) -> p b q r", b=BATCHES, r=R)[:, :, 0:per - 1, R - 1])
                ins = nc.vector.memset(first[:, :, 0:1], 0.0)
            ins.then_inc(carry_ready, 1)
            phase_end(dve, 4)

            def second_pass(i, t, par):
                last, tl = 1 - par, t - 1 + par
                if inside(i, 4):
                    place(1, i - 4, t - 2, par)
                if inside(i, 3):
                    choose(1, i - 3, last)
                if inside(i, 1):
                    dve.wait_ge(x_loaded[last], XL_SECOND + 16 * (tl + 1))
                    for h in range(2):
                        dve.wait_ge(ssm_in_psum, 2 * (i - 1) + h + 1)
                        x_h = flat(x_in[:, last, 2 * h:2 * h + 2])
                        nc.vector.tensor_tensor(x_h, x_h, bank[6 + h][:], ALU.add).then_inc(x2_ready, 1)
                        wait_apart(dve, (x2_ready, 2 * (i - 1) + h + 1))
                        if h == 0:
                            norm_stats(last, range(0, 2))
                    norm(1, i - 1, last, range(2, R))
                    norm_end(1, i - 1)
                if inside(i, 1):
                    dve.wait_ge(rounded_in_ring, STEPS + i)
                    nc.vector.tensor_tensor(ring[:, tl, 1, last, :], raw_chunk[:, last],
                                            ring[:, tl, 0, last, :].bitcast(F32),
                                            ALU.subtract).then_inc(experts_split, 8)
                if inside(i, 0):
                    dve.wait_ge(e_loaded[par], 16 * (t + 1))
                    dve.wait_ge(c_ready, i + 1)
                    nc.vector.tensor_tensor(flat(e_in[:, par]), flat(e_in[:, par]), flat(c_sb[:, par]),
                                            ALU.add).then_inc(s_ready, 1)

            run_steps(dve, second_pass, STEPS + 3, first=4)
            routed(1)
            phase_end(dve, 5)
            experts(1)
            phase_end(dve, 6)

            def last_pass(i, t, par):
                dve.wait_ge(x_loaded[par], XL_LAST + 16 * (t + 1))
                dve.wait_ge(pair_loaded[par], 8 * STEPS + 16 * (t + 1))
                add_pairs(i, par, STEPS + i).then_inc(out_ready, 1)

            run_steps(dve, last_pass)


_INS = ['L0_attn_x', 'L0_attn_W_u', 'L0_attn_b_u', 'L0_attn_W_g', 'L0_attn_b_g', 'L0_attn_A', 'L0_attn_Bm',
        'L0_attn_Cm', 'L0_attn_D', 'L0_ffn_router_w', 'L0_ffn_gate_w', 'L0_ffn_up_w', 'L0_ffn_down_w']
_OUTS = [((4, 2048, 256), 'float32')]


def kernel(**inputs):
    import numpy as _np
    import concourse.bacc as _bacc
    from concourse import mybir as _mybir
    from concourse.bass_utils import run_bass_kernel_spmd as _run

    nc = _bacc.Bacc("TRN2", target_bir_lowering=False, num_devices=1)
    arrays, args = {}, []
    for name in _INS:
        a = _np.ascontiguousarray(inputs[name])
        arrays[f"in_{name}_dram"] = a
        args.append(nc.dram_tensor(f"in_{name}_dram", a.shape, _mybir.dt.from_np(a.dtype), kind="ExternalInput").ap())
    for i, (shape, dtype) in enumerate(_OUTS):
        dt = _mybir.dt.from_np(_np.dtype(dtype))
        args.append(nc.dram_tensor(f"out_{i}_dram", shape, dt, kind="ExternalOutput").ap())
    macaron(nc, *args)
    r = _run(nc, [arrays], core_ids=[0])
    return r.results[0]["out_0_dram"]
```
